# Optimizing a Trainium2 kernel written in Bass

```python
import numpy as np
import jax
import jax.numpy as jnp

def _softmax(x, axis=-1):
    return jax.nn.softmax(x, axis=axis)

def _gelu(x):
    return jax.nn.gelu(x, approximate=True)

def _silu(x):
    return jax.nn.silu(x)

def _sigmoid(x):
    return jax.nn.sigmoid(x)

def _layernorm(x, axis=-1, eps=1e-05):
    m = jnp.mean(x, axis=axis, keepdims=True)
    v = jnp.var(x, axis=axis, keepdims=True)
    return (x - m) / jnp.sqrt(v + eps)

def _scatter_add(tgt, idx, src, axis=0):
    return tgt.at[idx].add(src)

def _segment_sum(src, seg, n):
    return jax.ops.segment_sum(src, seg, n)
kernel_name = 'mk_seq_preln_d2_jaxref_r8_d94889'

def setup_inputs(seed: int=0):
    np.random.seed(seed)
    _w = jnp.asarray

    def _L0_attn_setup():
        import jax, jax.numpy as jnp
        import numpy as np
        B, T, D = (2, 512, 128)
        H, DK, DV, K = (16, 64, 128, 4)
        EPS = 1e-06

        def _causal_conv_silu(x, w):
            Kw = w.shape[1]
            xp = jnp.pad(x, ((0, 0), (Kw - 1, 0), (0, 0)))
            y = sum((w[:, j] * xp[:, j:j + x.shape[1], :] for j in range(Kw)))
            return jax.nn.silu(y)

        def _l2_norm(x, eps=EPS):
            n = jnp.sqrt(jnp.sum(x * x, axis=-1, keepdims=True))
            return x / jnp.maximum(n, eps)

        def _rms_norm(x, eps=EPS):
            x32 = x.astype(jnp.float32)
            ms = jnp.mean(x32 * x32, axis=-1, keepdims=True)
            return x32 * jax.lax.rsqrt(ms + eps)

        def _gdn_recurrence(q, k, v, alpha, beta):

            def step(S, inp):
                q_t, k_t, v_t, a_t, b_t = inp
                kS = jnp.einsum('bhd,bhdv->bhv', k_t, S)
                kkS = jnp.einsum('bhd,bhv->bhdv', k_t, kS)
                S = a_t[..., None, None] * (S - b_t[..., None, None] * kkS) + jnp.einsum('bhd,bhv->bhdv', k_t, v_t)
                o_t = jnp.einsum('bhdv,bhd->bhv', S, q_t)
                return (S, o_t)
            S0 = jnp.zeros((q.shape[0], H, DK, DV), dtype=jnp.float32)
            tm = lambda a: jnp.moveaxis(a, 1, 0)
            S, o = jax.lax.scan(step, S0, (tm(q), tm(k), tm(v), tm(alpha), tm(beta)))
            return (jnp.moveaxis(o, 0, 1), S)
        key = jax.random.key(seed)
        ks = jax.random.split(key, 13)
        s = lambda d: 1.0 / np.sqrt(d)
        inp = {'x': jax.random.normal(ks[0], (B, T, D), dtype=jnp.float32), 'Wq': jax.random.normal(ks[1], (H * DK, D), dtype=jnp.float32) * s(D), 'Wk': jax.random.normal(ks[2], (H * DK, D), dtype=jnp.float32) * s(D), 'Wv': jax.random.normal(ks[3], (H * DV, D), dtype=jnp.float32) * s(D), 'Wb': jax.random.normal(ks[4], (H, D), dtype=jnp.float32) * s(D), 'Wa': jax.random.normal(ks[5], (H, D), dtype=jnp.float32) * s(D), 'A_log': jax.random.normal(ks[6], (H,), dtype=jnp.float32) * 0.5, 'dt_bias': jax.random.normal(ks[7], (H,), dtype=jnp.float32) * 0.5, 'Wo': jax.random.normal(ks[8], (D, H * DV), dtype=jnp.float32) * s(H * DV), 'conv_q': jax.random.normal(ks[9], (H * DK, K), dtype=jnp.float32) * s(K), 'conv_k': jax.random.normal(ks[10], (H * DK, K), dtype=jnp.float32) * s(K), 'conv_v': jax.random.normal(ks[11], (H * DV, K), dtype=jnp.float32) * s(K)}
        return inp
    _L0_attn_in = _L0_attn_setup()

    def _L0_ffn_setup():
        import jax, jax.numpy as jnp
        import numpy as np
        key = jax.random.key(seed)
        kx, kw = jax.random.split(key)
        x = jax.random.normal(kx, (32, 512, 128), dtype=jnp.float32)
        weight = jax.random.normal(kw, (128, 128), dtype=jnp.float32) * 0.01
        return {'x': x, 'weight': weight}
    _L0_ffn_in = _L0_ffn_setup()

    def _L1_attn_setup():
        import jax, jax.numpy as jnp
        import numpy as np
        B, S, DIN, DIM = (1, 512, 128, 128)
        NH, NKV = (16, 4)
        HD = DIM // NH
        GS = NH // NKV
        key = jax.random.key(seed)
        ks = jax.random.split(key, 5)

        def w(k, shape, fan_in):
            return jax.random.normal(k, shape, jnp.float32) * fan_in ** (-0.5)
        return {'x': jax.random.normal(ks[0], (B, S, DIN), jnp.float32), 'wq': w(ks[1], (DIM, DIN), DIN), 'wk': w(ks[2], (NKV * HD, DIN), DIN), 'wv': w(ks[3], (NKV * HD, DIN), DIN), 'wo': w(ks[4], (DIM, DIM), DIM)}
    _L1_attn_in = _L1_attn_setup()

    def _L1_ffn_setup():
        import jax, jax.numpy as jnp
        import numpy as np
        B, L, D, E, K, DFF = (2, 256, 128, 8, 2, 512)
        key = jax.random.key(seed)
        kx, kr, kg, ku, kd = jax.random.split(key, 5)
        scale = 0.02
        return {'x': jax.random.normal(kx, (B, L, D), dtype=jnp.float32), 'Wr': jax.random.normal(kr, (E, D), dtype=jnp.float32) * scale, 'Wg': jax.random.normal(kg, (E, DFF, D), dtype=jnp.float32) * scale, 'Wu': jax.random.normal(ku, (E, DFF, D), dtype=jnp.float32) * scale, 'Wd': jax.random.normal(kd, (E, D, DFF), dtype=jnp.float32) * scale}
    _L1_ffn_in = _L1_ffn_setup()
    _d = {'L0_attn_x': _L0_attn_in['x'], 'L0_attn_Wq': _L0_attn_in['Wq'], 'L0_attn_Wk': _L0_attn_in['Wk'], 'L0_attn_Wv': _L0_attn_in['Wv'], 'L0_attn_Wb': _L0_attn_in['Wb'], 'L0_attn_Wa': _L0_attn_in['Wa'], 'L0_attn_A_log': _L0_attn_in['A_log'], 'L0_attn_dt_bias': _L0_attn_in['dt_bias'], 'L0_attn_Wo': _L0_attn_in['Wo'], 'L0_attn_conv_q': _L0_attn_in['conv_q'], 'L0_attn_conv_k': _L0_attn_in['conv_k'], 'L0_attn_conv_v': _L0_attn_in['conv_v'], 'L0_ffn_weight': _L0_ffn_in['weight'], 'L1_attn_wq': _L1_attn_in['wq'], 'L1_attn_wk': _L1_attn_in['wk'], 'L1_attn_wv': _L1_attn_in['wv'], 'L1_attn_wo': _L1_attn_in['wo'], 'L1_ffn_Wr': _L1_ffn_in['Wr'], 'L1_ffn_Wg': _L1_ffn_in['Wg'], 'L1_ffn_Wu': _L1_ffn_in['Wu'], 'L1_ffn_Wd': _L1_ffn_in['Wd']}
    _x0 = _d['L0_attn_x']
    _d['L0_attn_x'] = jax.random.normal(jax.random.fold_in(jax.random.key(seed), 1), (8, 256, 128), dtype=_x0.dtype)
    del _x0
    return _d

def reference(L0_attn_x, L0_attn_Wq, L0_attn_Wk, L0_attn_Wv, L0_attn_Wb, L0_attn_Wa, L0_attn_A_log, L0_attn_dt_bias, L0_attn_Wo, L0_attn_conv_q, L0_attn_conv_k, L0_attn_conv_v, L0_ffn_weight, L1_attn_wq, L1_attn_wk, L1_attn_wv, L1_attn_wo, L1_ffn_Wr, L1_ffn_Wg, L1_ffn_Wu, L1_ffn_Wd):

    def _L0_attn_ref(x, Wq, Wk, Wv, Wb, Wa, A_log, dt_bias, Wo, conv_q, conv_k, conv_v):
        import jax, jax.numpy as jnp
        import numpy as np
        B, T, D = (2, 512, 128)
        H, DK, DV, K = (16, 64, 128, 4)
        EPS = 1e-06

        def _causal_conv_silu(x, w):
            Kw = w.shape[1]
            xp = jnp.pad(x, ((0, 0), (Kw - 1, 0), (0, 0)))
            y = sum((w[:, j] * xp[:, j:j + x.shape[1], :] for j in range(Kw)))
            return jax.nn.silu(y)

        def _l2_norm(x, eps=EPS):
            n = jnp.sqrt(jnp.sum(x * x, axis=-1, keepdims=True))
            return x / jnp.maximum(n, eps)

        def _rms_norm(x, eps=EPS):
            x32 = x.astype(jnp.float32)
            ms = jnp.mean(x32 * x32, axis=-1, keepdims=True)
            return x32 * jax.lax.rsqrt(ms + eps)

        def _gdn_recurrence(q, k, v, alpha, beta):

            def step(S, inp):
                q_t, k_t, v_t, a_t, b_t = inp
                kS = jnp.einsum('bhd,bhdv->bhv', k_t, S)
                kkS = jnp.einsum('bhd,bhv->bhdv', k_t, kS)
                S = a_t[..., None, None] * (S - b_t[..., None, None] * kkS) + jnp.einsum('bhd,bhv->bhdv', k_t, v_t)
                o_t = jnp.einsum('bhdv,bhd->bhv', S, q_t)
                return (S, o_t)
            S0 = jnp.zeros((q.shape[0], H, DK, DV), dtype=jnp.float32)
            tm = lambda a: jnp.moveaxis(a, 1, 0)
            S, o = jax.lax.scan(step, S0, (tm(q), tm(k), tm(v), tm(alpha), tm(beta)))
            return (jnp.moveaxis(o, 0, 1), S)
        Bx, Tx = (x.shape[0], x.shape[1])
        q = _causal_conv_silu(x @ Wq.T, conv_q).reshape(Bx, Tx, H, DK)
        k = _causal_conv_silu(x @ Wk.T, conv_k).reshape(Bx, Tx, H, DK)
        v = _causal_conv_silu(x @ Wv.T, conv_v).reshape(Bx, Tx, H, DV)
        q = _l2_norm(q)
        k = _l2_norm(k)
        a_lin = (x @ Wa.T).astype(jnp.float32)
        alpha = jnp.exp(-jnp.exp(A_log) * jax.nn.softplus(a_lin + dt_bias))
        beta = 2.0 * jax.nn.sigmoid(x @ Wb.T)
        o, _S = _gdn_recurrence(q.astype(jnp.float32), k.astype(jnp.float32), v.astype(jnp.float32), alpha, beta)
        o = _rms_norm(o).astype(x.dtype).reshape(Bx, Tx, H * DV)
        return o @ Wo.T

    def _L0_ffn_ref(x, weight):
        import jax, jax.numpy as jnp
        import numpy as np
        b_weight = jnp.sign(weight)
        return jnp.einsum('bsi,oi->bso', x, b_weight)

    def _L1_attn_ref(x, wq, wk, wv, wo):
        import jax, jax.numpy as jnp
        import numpy as np
        B, S, DIN, DIM = (1, 512, 128, 128)
        NH, NKV = (16, 4)
        HD = DIM // NH
        GS = NH // NKV
        b, s, _ = x.shape
        q = (x @ wq.T).reshape(b, s, NKV, GS, HD)
        k = (x @ wk.T).reshape(b, s, NKV, HD)
        v = (x @ wv.T).reshape(b, s, NKV, HD)
        scale = jnp.asarray(HD ** 0.5, x.dtype)
        att = jnp.einsum('bsgmd,btgd->bgmst', q, k) / scale
        causal = jnp.triu(jnp.ones((s, s), bool), 1)
        att = jnp.where(causal, -jnp.inf, att)
        att = jax.nn.softmax(att, axis=-1)
        ctx = jnp.einsum('bgmst,btgd->bsgmd', att, v).reshape(b, s, DIM)
        return ctx @ wo.T

    def _L1_ffn_ref(x, Wr, Wg, Wu, Wd):
        import jax, jax.numpy as jnp
        import numpy as np
        B, L, D, E, K, DFF = (2, 256, 128, 8, 2, 512)
        Bb, Ll, Dd = x.shape
        T = Bb * Ll
        xt = x.reshape(T, Dd)
        logits = jnp.einsum('td,ed->te', xt, Wr)
        scores = jax.nn.softmax(logits, axis=-1)
        k_scores, k_ids = jax.lax.top_k(scores, K)
        eps = jnp.finfo(x.dtype).eps
        k_w = k_scores / (k_scores.sum(axis=-1, keepdims=True) + eps)
        combine = jnp.sum(jax.nn.one_hot(k_ids, E, dtype=x.dtype) * k_w[..., None], axis=1)
        g = jnp.einsum('td,efd->etf', xt, Wg)
        u = jnp.einsum('td,efd->etf', xt, Wu)
        h = jax.nn.relu(g) * u
        out_e = jnp.einsum('etf,edf->etd', h, Wd)
        out = jnp.einsum('te,etd->td', combine, out_e)
        return out.reshape(Bb, Ll, Dd)
    x = L0_attn_x
    x = x + _L0_attn_ref(_layernorm(x, axis=-1), L0_attn_Wq, L0_attn_Wk, L0_attn_Wv, L0_attn_Wb, L0_attn_Wa, L0_attn_A_log, L0_attn_dt_bias, L0_attn_Wo, L0_attn_conv_q, L0_attn_conv_k, L0_attn_conv_v)
    x = x + _L0_ffn_ref(_layernorm(x, axis=-1), L0_ffn_weight)
    x = x + _L1_attn_ref(_layernorm(x, axis=-1), L1_attn_wq, L1_attn_wk, L1_attn_wv, L1_attn_wo)
    x = x + _L1_ffn_ref(_layernorm(x, axis=-1), L1_ffn_Wr, L1_ffn_Wg, L1_ffn_Wu, L1_ffn_Wd)
    return x

_drawn_inputs = setup_inputs


def setup_inputs(seed=0):
    import zlib

    import numpy as np

    out = dict(_drawn_inputs(seed))
    spreads = {}
    factors = {'L1_attn_wq': 3.449,
     'L1_attn_wk': 3.567,
     'L1_ffn_Wr': 8.0,
     'L1_ffn_Wg': 8.0,
     'L1_ffn_Wu': 8.0,
     'L1_ffn_Wd': 8.0}
    for name, (base, spread) in spreads.items():
        noise = np.random.default_rng([zlib.crc32(name.encode()), seed]).standard_normal(out[name].shape)
        drawn = base * np.exp(spread * noise) if base else spread * noise
        out[name] = jnp.asarray(drawn.astype(out[name].dtype))
    for name, factor in factors.items():
        out[name] = (out[name] * factor).astype(out[name].dtype)
    return out
```

```python
import concourse.bass as bass
from concourse import mybir
from contextlib import ExitStack

F32 = mybir.dt.float32
BF16 = mybir.dt.bfloat16
ALU = mybir.AluOpType
ACT = mybir.ActivationFunctionType
AX = mybir.AxisListType

NB, T, D = 8, 256, 128
H, DK, DV = 16, 64, 128
NE, DFF = 8, 512
NP = NB // 2
NT = 16
GH = 2
NG = H // GH
NJ = GH * 4


class Done:

    def __init__(self):
        self.used = False
        self.sem = None
        self.value = 0


class Queue:

    def __init__(self, sem):
        self.sem = sem
        self.items = []

    def put(self, fn, waits, dma_sem=None, count=0):
        for w in waits:
            if w is not None:
                w.used = True
        d = Done()
        if dma_sem is not None:
            d.sem, d.value = dma_sem, count
        self.items.append((fn, waits, d, 1 if dma_sem is None else 16))
        return d

    def number(self):
        n = 0
        for _, _, d, step in self.items:
            if step == 1 and d.used:
                n += 1
                d.sem, d.value = self.sem, n

    def emit(self, eng):
        seen = {}
        for fn, waits, d, step in self.items:
            for w in waits:
                if w is not None and seen.get(id(w.sem), 0) < w.value:
                    eng.wait_ge(w.sem, w.value)
                    seen[id(w.sem)] = w.value
            ins = fn(eng)
            if step == 16 or d.used:
                ins.then_inc(d.sem, step)


class Bufs:

    def __init__(self, bufs):
        self.free = [(b, ()) for b in bufs]

    def take(self):
        return self.free.pop(0)

    def give(self, b, *dones):
        self.free.append((b, dones))


def program(nc, x_d, wqkv_d, conv_d, wab_d, gate_d, wo_d, sgn_d, awq_d, awk_d, awv_d, awo_d,
            wr_d, wg_d, wu_d, wd_d, ident_d, idp_d, emask_d, lmask_d, sel_d, reset_d, tri_d, out_d):
    with ExitStack() as ctx:
        def sb(name, shape, dt=F32):
            return ctx.enter_context(nc.sbuf_tensor(name, shape, dt))

        def sem(name):
            return ctx.enter_context(nc.semaphore(name))

        pe, act, dve, pool, sp = (Queue(sem(f"s_{n}")) for n in ("pe", "act", "dve", "pool", "sp"))

        def mm(out, l, r, *waits, start=True, stop=True, shared=False):
            return pe.put(lambda e: e.matmul(out, l, r, start=start, stop=stop, skip_group_check=shared), waits)

        def tr(out, a, i, *waits):
            return pe.put(lambda e: e.transpose(out, a, i), waits)

        def ac(out, a, f, *waits, scale=1.0, bias=0.0):
            return act.put(lambda e: e.activation(out, a, f, scale=scale, bias=bias), waits)

        def tt(out, a, b, op, *waits, q=dve):
            return q.put(lambda e: e.tensor_tensor(out, a, b, op), waits)

        def ts(out, a, s1, s2, op0, op1, *waits):
            if op1 is None:
                return dve.put(lambda e: e.tensor_scalar(out, a, s1, None, op0), waits)
            return dve.put(lambda e: e.tensor_scalar(out, a, s1, s2, op0, op1), waits)

        def stt(out, a, s, b, op0, op1, *waits):
            return dve.put(lambda e: e.scalar_tensor_tensor(out, a, s, b, op0, op1), waits)

        def cp(out, a, *waits, q=dve):
            return q.put(lambda e: e.tensor_copy(out, a), waits)

        def fill(out, v, *waits, q=dve):
            return q.put(lambda e: e.memset(out, v), waits)

        def vtr(out, a, *waits):
            return dve.put(lambda e: e.transpose(out, a), waits)

        def red(out, a, op, *waits):
            return dve.put(lambda e: e.tensor_reduce(out, a, AX.X, op), waits)

        nload = [0]

        def load(dst, src, *waits):
            nload[0] += 1
            return sp.put(lambda e: e.dma_start(dst, src), waits, sem(f"s_ld{nload[0]}"), 16)

        s_rows, s_out = [sem("s_rows0"), sem("s_rows1")], sem("s_out")
        count = {0: 0, 1: 0, "out": 0}

        banks = [ctx.enter_context(nc.psum_tensor(f"bank{i}", [128, 512], F32)) for i in range(8)]
        PS = Bufs(banks)

        X = sb("X", [128, NT, 128])
        ident = sb("ident", [128, 128])
        identb = sb("identb", [128, 128], BF16)
        idp = sb("idp", [128, 1, 64])
        emask = sb("emask", [128, 256])
        emaskb = sb("emaskb", [128, 2, 128], BF16)
        lmask = sb("lmask", [128, 6, 64])
        sel = sb("sel", [128, 8, 16])
        wab = sb("wab", [128, 32])
        gate = sb("gate", [16, 4])
        cst = sb("cst", [128, 2])
        conv = sb("conv", [128, 32, 4])
        reset = sb("reset", [16, 512])
        WQ = sb("WQ", [128, 6144])
        wqkv = WQ[:, 0:4096]
        wo = WQ[:, 4096:6144].rearrange("p (h d) -> p h d", h=H)

        l_x = load(X[:, :, :], x_d.rearrange("b (c p) d -> p (b c) d", p=128))
        l_id = load(ident[:, :], ident_d)
        l_wq = load(wqkv, wqkv_d)
        l_cv = load(conv[:, :, :], conv_d)
        l_wab = load(wab[:, :], wab_d)
        l_gate = load(gate[:, 0:2], gate_d)
        l_sel = load(sel[:, :, :], sel_d)
        l_em = load(emask[:, :], emask_d)
        l_idp = load(idp[:, 0, :], idp_d)
        l_lm = load(lmask[:, :, :], lmask_d)
        l_rs = load(reset[:, :], reset_d)
        l_wo = load(wo, wo_d)

        c_idb = cp(identb[:, :], ident[:, :], l_id)
        c_emb = cp(emaskb[:, :, :], emask[:, :].rearrange("p (k t) -> p k t", k=2), l_em)
        c_cv = ts(conv[:, :, :], conv[:, :, :], 0.5, None, ALU.mult, None, l_cv)
        c_one = fill(cst[:, 0:1], 1.0)
        g_e = ac(gate[:, 2:3], gate[:, 0:1], ACT.Exp, l_gate)
        g_n = ts(gate[:, 3:4], gate[:, 2:3], -1.0, None, ALU.mult, None, g_e)

        KQ = sb("KQ", [128, 8, 2, 2, 256])
        AMt = sb("AM", [128, 2, GH, 2, 768])
        ETt = sb("ET", [128, 3, 512])
        YFt = sb("YF", [128, 2, NJ, 128])
        YPt = sb("YP", [128, 2, NJ, 64])
        XPt = sb("XP", [128, 2, NJ, 64])
        PPt = sb("PP", [128, 2, NJ, 64])
        Vt = sb("V", [128, 2, GH, 4, 128])
        Ut = sb("U", [128, 2, GH, 4, 128])
        OTb = sb("OT", [128, 2, GH, 512])
        yp_t = sb("yp_t", [128, 3, 2, 259])
        cv_t = sb("cv_t", [128, 2, 512])
        sq_t = sb("sq_t", [128, 2, 512])
        vt_t = sb("vt_t", [128, 2, 512])
        xn = sb("xn", [128, 4, 128])
        xnT = sb("xnT", [128, 512])
        st6 = sb("st6", [128, 4, 6])
        mv = sb("mv", [128, 4, 2])
        rs = sb("rs", [128, 4, 2])
        gt = sb("gt", [16, 6, 512])
        spl = sb("spl", [16, 9, 512], BF16)
        CRt = sb("CR", [6, 2, GH, 512], BF16)
        DRt = sb("DR", [6, 2, GH, 2, 2, 256], BF16)
        LQ = sb("LQ", [128, 4, H])
        E2 = sb("E2", [128, 4, H])
        RR = sb("RR", [128, 4, 4, GH])

        YPAD = Bufs([yp_t[:, i, :, :] for i in range(3)])
        CV = Bufs([cv_t[:, i, :] for i in range(2)])
        SQ = Bufs([sq_t[:, i, :] for i in range(2)])
        VT = Bufs([vt_t[:, i, :] for i in range(2)])
        ETR = Bufs([ETt[:, i, :] for i in range(3)])

        z_pad = fill(yp_t[:, :, :, 0:3], 0.0)
        z_yf = fill(YFt[:, :, :, :], 0.0)
        z_cr = fill(CRt[:, :, :, :], 1.0)
        z_dr = fill(DRt[:, :, :, :, :, :], 1.0)

        f = {}
        x_w = [l_x] * NT

        def norm(tiles, dst, *free):
            n = len(tiles)
            for k, t in enumerate(tiles):
                d = dve.put(lambda e, o=st6[:, k, :], a=X[:, t, :]: e.bn_stats(o, a), (x_w[t], f.get("st")))
            for k in range(n):
                d2 = dve.put(lambda e, o=mv[:, k, :], a=st6[:, k, :]: e.bn_aggr(o, a), (d,))
            d = ts(rs[:, 0:n, 0], mv[:, 0:n, 1], 1e-5, None, ALU.add, None, d2)
            d = ac(rs[:, 0:n, 1], rs[:, 0:n, 0], ACT.Ln, d)
            d = ac(rs[:, 0:n, 0], rs[:, 0:n, 1], ACT.Exp, d, scale=-0.5)
            for k, t in enumerate(tiles):
                d2 = ts(dst[:, k, :], X[:, t, :], mv[:, k, 0:1], rs[:, k, 0:1], ALU.subtract, ALU.mult, d, *free)
            f["st"] = d2
            return d2

        def transposed(src, dst, n, ready, *free):
            b, fr = PS.take()
            for k in range(n):
                d = tr(b[:, k * 128:(k + 1) * 128], src[:, k, :], ident[:, :], ready, l_id, *fr)
            r = ac(dst[:, 0:n * 128], b[:, 0:n * 128], ACT.Copy, d, *free)
            PS.give(b, r)
            return r, d

        def silu_tile(ct, dst, x_r, *free):
            b, fr = PS.take()
            m = mm(b[:, :], wqkv[:, ct * 128:(ct + 1) * 128], xnT[:, :], x_r, l_wq, *fr)
            y, yfr = YPAD.take()
            r = ac(y[:, :, 3:259], b[:, :].rearrange("p (b t) -> p b t", b=2), ACT.Copy, m, z_pad, *yfr)
            PS.give(b, r)
            c, cfr = CV.take()
            c2 = c.rearrange("p (b t) -> p b t", b=2)
            d = ts(c2, y[:, :, 0:256], conv[:, ct, 0:1], None, ALU.mult, None, r, c_cv, *cfr)
            for j in range(1, 4):
                d = stt(c2, y[:, :, j:j + 256], conv[:, ct, j:j + 1], c2, ALU.mult, ALU.add, d)
            t = y[:, :, 3:259]
            r = ac(t, c2, ACT.Tanh, d)
            d = stt(dst, t, 1.0, c2, ALU.add, ALU.mult, r, *free)
            CV.give(c, d)
            YPAD.give(y, d)
            return d, m

        ready = {}

        def prep(p):
            d = norm([4 * p + k for k in range(4)], xn[:, :, :], f.get("xn"))
            x_r, f["xn"] = transposed(xn, xnT, 4, d, f.get("xnT"), f.get("xnT2"))
            ready["x", p] = x_r
            yield
            nk, nkf = PS.take()
            nq, nqf = PS.take()
            for i8 in range(8):
                for kq, nbank, nfr in ((0, nk, nkf), (1, nq, nqf)):
                    d, _ = silu_tile((1 - kq) * 8 + i8, KQ[:, i8, :, kq, :], x_r, f.get(("kq", i8)))
                    ready["kq", p, i8] = d
                    q, qfr = SQ.take()
                    s = ac(q.rearrange("p (b t) -> p b t", b=2), KQ[:, i8, :, kq, :], ACT.Square, d, *qfr)
                    dn = mm(nbank[0:16, :], sel[:, i8, :], q, s, l_sel, *nfr, start=i8 == 0, stop=i8 == 7)
                    SQ.give(q, dn)
                    if kq == 0:
                        dnk = dn
                yield
            G = lambda k: gt[:, k, :]
            ab, afr = PS.take()
            bb, bfr = PS.take()
            da = mm(ab[0:16, :], wab[:, 0:16], xnT[:, :], l_wab, x_r, *afr)
            db = mm(bb[0:16, :], wab[:, 16:32], xnT[:, :], l_wab, *bfr)
            f["xnT"] = db
            d = ts(G(0), ab[0:16, :], gate[:, 1:2], None, ALU.add, None, da, g_n, f.get("spl"))
            PS.give(ab, d)
            d = ac(G(1), G(0), ACT.Abs, d)
            d = ac(G(1), G(1), ACT.Exp, d, scale=-1.0)
            d = ac(G(1), G(1), ACT.Ln, d, c_one, bias=cst[0:16, 0:1])
            d = stt(G(1), G(0), 0.0, G(1), ALU.max, ALU.add, d)
            d = ts(G(1), G(1), gate[:, 3:4], None, ALU.mult, None, d)
            d_g = dve.put(lambda e: e.tensor_tensor_scan(G(2), reset[:, :], G(1), 0.0, ALU.mult, ALU.add), (d, l_rs))
            d = ac(G(3), bb[0:16, :], ACT.Abs, db)
            d = ac(G(3), G(3), ACT.Exp, d, scale=-1.0)
            d = ac(G(3), G(3), ACT.Ln, d, bias=cst[0:16, 0:1])
            d_b = stt(G(3), bb[0:16, :], 0.0, G(3), ALU.min, ALU.subtract, d)
            PS.give(bb, d_b)
            yield
            d1 = ts(G(4), nk[0:16, :], 1e-12, None, ALU.max, None, dnk)
            d2 = ts(G(5), nq[0:16, :], 1e-12, None, ALU.max, None, dn, f.get("lqT"))
            PS.give(nk, d1)
            PS.give(nq, d2)
            d1 = ac(G(4), G(4), ACT.Ln, d1)
            d2 = ac(G(5), G(5), ACT.Ln, d2)
            dc = stt(G(0), G(4), -0.5, G(2), ALU.mult, ALU.subtract, d1, d_g)
            d = stt(G(1), G(4), -0.5, G(2), ALU.mult, ALU.add, d_g)
            dd = stt(G(1), G(3), 0.6931471805599453, G(1), ALU.add, ALU.add, d, d_b)
            lq_r = ts(G(5), G(5), -0.5, None, ALU.mult, None, d2)
            for k, (src, dn) in enumerate(((0, dc), (1, dd), (2, d_g))):
                d = cp(spl[:, 3 * k, :], G(src), dn, dd, f.get(("rows", 0)), f.get(("rows", 1)), q=pool)
                d = tt(G(3), G(src), spl[:, 3 * k, :], ALU.subtract, d, q=pool)
                d = cp(spl[:, 3 * k + 1, :], G(3), d, q=pool)
                d = tt(spl[:, 3 * k + 2, :], G(3), spl[:, 3 * k + 1, :], ALU.subtract, d, q=pool)
            f["spl"] = d
            ready["spl", p] = d
            yield
            lb, lfr = PS.take()
            for k in range(4):
                d = tr(lb[:, k * 16:(k + 1) * 16], G(5)[:, k * 128:(k + 1) * 128], ident[0:16, 0:16], lq_r, *lfr)
            f["lqT"] = d
            d = cp(LQ[:, :, :], lb[:, 0:64].rearrange("p (t h) -> p t h", t=4), d, f.get("rr"))
            PS.give(lb, d)
            ready["e2", p] = ac(E2[:, :, :], LQ[:, :, :], ACT.Exp, d, f.get("rr"), scale=2.0)

        def rows(p, g, sl, CR, DR):
            hs = slice(g * GH, g * GH + GH)
            for k in range(3):
                for r in range(3):
                    if k == 0:
                        dst, src = CR[r:r + 1, :, :], spl[hs, r, :]
                    else:
                        dst = DR[3 + r:4 + r, :, :, k - 1, :]
                        src = spl[hs, 3 * k + r, :].rearrange("h (b t) -> h b t", b=2)
                    count[sl] += 16
                    d = sp.put(lambda e, dst=dst, src=src: e.dma_start(dst, src),
                               (ready["spl", p], z_cr, z_dr, f.get(("ex", sl)), f.get(("rows", sl))), s_rows[sl], count[sl])
            f["rows", sl] = d
            return d

        def group(p, g, sl):
            AM, YF, YP, XP, PP, V, U, OTt = (a[:, sl] for a in (AMt, YFt, YPt, XPt, PPt, Vt, Ut, OTb))
            x_r = ready["x", p]
            CR, DR = CRt[:, sl], DRt[:, sl]
            rows_r = rows(p, g, sl, CR, DR)
            for hh in range(GH):
                vt, vfr = VT.take()
                d, f["xnT2"] = silu_tile(16 + g * GH + hh, vt.rearrange("p (b t) -> p b t", b=2), x_r, *vfr)
                b, fr = PS.take()
                for k in range(4):
                    d2 = tr(b[:, k * 128:(k + 1) * 128], vt[:, k * 128:(k + 1) * 128], ident[:, :], d, *fr)
                VT.give(vt, d2)
                v_r = ac(V[:, hh, :, :], b[:, :].rearrange("p (t n) -> p t n", t=4), ACT.Copy, d2, f.get(("u", sl)))
                PS.give(b, v_r)
                yield
            for hh in range(GH):
                h = g * GH + hh
                i8, hp = h // 2, 64 * (h % 2)
                for part in range(3):
                    eb, efr = PS.take()
                    kb, kfr = PS.take()
                    spans = [(part, 0, 0, 512)] if part < 2 else [(0, 128, 0, 256), (1, 128, 256, 256)]
                    for n, (b, s0, o, w) in enumerate(spans):
                        e3 = eb[:, o:o + w].rearrange("p (k t) -> p k t", k=2)
                        k3 = kb[:, o:o + w].rearrange("p (k t) -> p k t", k=2)
                        mm(e3, CR[0:6, hh, b * 256 + s0:b * 256 + s0 + 128], DR[0:6, hh, b, :, s0:256],
                           rows_r, *efr, start=n == 0, stop=False, shared=True)
                        de = mm(e3[:, :, 0:128], identb[:, :], emaskb[:, :, :], c_emb, c_idb,
                                start=False, stop=True, shared=True)
                        dk = mm(k3, KQ[hp:hp + 64, i8, b, 0, s0:s0 + 128], KQ[hp:hp + 64, i8, b, :, s0:256],
                                ready["kq", p, i8], *kfr)
                    f["ex", sl] = de
                    if h % 2:
                        f["kq", i8] = dk
                    et, tfr = ETR.take()
                    r = ac(et, eb[:, :], ACT.Exp, de, *tfr)
                    PS.give(eb, r)
                    if part < 2:
                        dst = AM[:, hh, part, :].rearrange("p (c n) -> p c n", c=3)[:, 0:3:2, :]
                    else:
                        dst = AM[:, hh, :, 256:512]
                    am_r = tt(dst, kb[:, :].rearrange("p (k t) -> p k t", k=2), et.rearrange("p (k t) -> p k t", k=2),
                              ALU.mult, dk, r, f.get(("am", sl)))
                    PS.give(kb, am_r)
                    ETR.give(et, am_r)
                    yield
            N4 = AM.rearrange("p h b (c n) -> p (h b) c n", c=3)
            N = lambda j, q, a: N4[64 * q:64 * q + 64, j // 2, j % 2, a:a + 64]
            W = lambda b: b[:, :].rearrange("p (j n) -> p j n", j=NJ)
            mask = lambda lv, q=slice(0, 128): lmask[q, lv:lv + 1, :].to_broadcast([q.stop - q.start, NJ, 64])
            for q in range(2):
                pq = slice(64 * q, 64 * q + 64)
                d = tt(YP[pq].rearrange("p (m c) n -> p m c n", c=2), N4[pq, :, 0:2, 64 * q:64 * q + 64],
                       mask(0, pq).rearrange("p (m c) n -> p m c n", c=2), ALU.mult, am_r, l_lm, f.get(("yf", sl)),
                       f.get(("inv", sl)))
            y_r = tt(YP[:, :, :], idp[:, :, :].to_broadcast([128, NJ, 64]), YP[:, :, :], ALU.subtract, d, l_idp)
            x_i = vtr(XP[:, :, :], YP[:, :, :], y_r, f.get(("inv", sl)))
            yield
            pp_f = f.get(("inv", sl))
            for lv in range(1, 6):
                b, fr = PS.take()
                for j in range(NJ):
                    for q in range(2):
                        pq = slice(64 * q, 64 * q + 64)
                        d = mm(b[pq, j * 64:j * 64 + 64], N(j, q, 64 * q), XP[pq, j, :], x_i, am_r, *fr)
                r = tt(PP[:, :, :], W(b), mask(lv), ALU.mult, d, pp_f)
                PS.give(b, r)
                yield
                b, fr = PS.take()
                for j in range(NJ):
                    for q in range(2):
                        pq = slice(64 * q, 64 * q + 64)
                        d = mm(b[pq, j * 64:j * 64 + 64], PP[pq, j, :], YP[pq, j, :], r, y_r, *fr)
                if lv == 5:
                    b2, fr2 = PS.take()
                    for j in range(NJ):
                        dx = mm(b2[0:64, j * 64:j * 64 + 64], YP[0:64, j, :], PP[0:64, j, :], *fr2)
                    d = dx
                pp_f = d
                y_r = tt(YP[:, :, :], YP[:, :, :], W(b), ALU.subtract, d)
                PS.give(b, y_r)
                if lv < 5:
                    x_i = vtr(XP[:, :, :], YP[:, :, :], y_r)
                else:
                    x_i = tt(XP[0:64], XP[0:64], W(b2)[0:64], ALU.subtract, dx)
                    PS.give(b2, x_i)
                yield
            b, fr = PS.take()
            for j in range(NJ):
                d = mm(b[64:128, j * 64:j * 64 + 64], N(j, 0, 64), XP[0:64, j, :], x_i, *fr)
            r = ts(PP[64:128], W(b)[64:128], -1.0, None, ALU.mult, None, d, pp_f)
            PS.give(b, r)
            r0 = cp(YF[0:64, :, 0:64], YP[0:64], y_r, z_yf, f.get(("yf", sl)), q=pool)
            r1 = cp(YF[64:128, :, 64:128], YP[64:128], y_r, z_yf, f.get(("yf", sl)), q=pool)
            yield
            b, fr = PS.take()
            for j in range(NJ):
                d = mm(b[0:64, j * 64:j * 64 + 64], PP[64:128, j, :], YP[64:128, j, :], r, y_r, *fr)
            f["inv", sl] = d
            r = ac(YF[0:64, :, 64:128], W(b)[0:64], ACT.Copy, d, z_yf, f.get(("yf", sl)))
            PS.give(b, r)
            yield

            def solve(c, *waits):
                b, fr = PS.take()
                for k in range(2 * GH):
                    d = mm(b[:, k * 128:(k + 1) * 128], YF[:, 2 * k + c, :], V[:, k // 2, 2 * (k % 2) + c, :], *waits, *fr)
                r = ac(U[:, :, c:4:2, :], b[:, :].rearrange("p (h b n) -> p h b n", h=GH, b=2), ACT.Copy, d, f.get(("o", sl)))
                PS.give(b, r)
                return r, d
            u1, _ = solve(0, r, r0, r1, v_r)
            yield
            b, fr = PS.take()
            for k in range(2 * GH):
                d = mm(b[:, k * 128:(k + 1) * 128], AM[:, k // 2, k % 2, 128:256], U[:, k // 2, 2 * (k % 2), :], u1, *fr)
            r = tt(V[:, :, 1:4:2, :], V[:, :, 1:4:2, :], b[:, :].rearrange("p (h b n) -> p h b n", h=GH, b=2),
                   ALU.subtract, d)
            PS.give(b, r)
            yield
            u2, d = solve(1, r)
            f["u", sl] = f["yf", sl] = d
            yield
            sb_, sfr = PS.take()
            o_r = []
            for hh in range(GH):
                b, fr = PS.take()
                for bt in range(2):
                    mm(b[:, bt * 256:bt * 256 + 256], U[:, hh, 2 * bt, :], AM[:, hh, bt, 512:768], u1, u2, *fr,
                       start=True, stop=False, shared=True)
                    d = mm(b[:, bt * 256 + 128:bt * 256 + 256], U[:, hh, 2 * bt + 1, :], AM[:, hh, bt, 384:512],
                           start=False, stop=True, shared=True)
                q, qfr = SQ.take()
                r = ac(q, b[:, :], ACT.Square, d, *qfr)
                r1 = ac(OTt[:, hh, :], b[:, :], ACT.Copy, f.get(("ot", sl)))
                o_r.append(r1)
                PS.give(b, r1)
                for k in range(4):
                    d2 = mm(sb_[:, k * GH + hh:k * GH + hh + 1], q[:, k * 128:(k + 1) * 128], cst[:, 0:1], r, c_one, *sfr)
                SQ.give(q, d2)
            f["am", sl] = f["o", sl] = d
            yield
            hs = slice(g * GH, g * GH + GH)
            A = lambda k: RR[:, k, :, :]
            d = tt(A(0), sb_[:, 0:4 * GH].rearrange("p (t h) -> p t h", t=4), E2[:, :, hs], ALU.mult,
                   d2, ready["e2", p])
            PS.give(sb_, d)
            d = ts(A(1), A(0), 1.0 / 128, 1e-6, ALU.mult, ALU.add, d)
            d = ac(A(2), A(1), ACT.Ln, d)
            d = stt(A(0), A(2), -0.5, LQ[:, :, hs], ALU.mult, ALU.add, d)
            r_r = ac(A(3), A(0), ACT.Exp, d, f.get("rr"))
            for hh in range(GH):
                b, fr = PS.take()
                for k in range(4):
                    d = mm(b[:, k * 128:(k + 1) * 128], OTt[:, hh, k * 128:(k + 1) * 128], wo[:, g * GH + hh, :],
                           o_r[hh], l_wo, *fr)
                for k in range(4):
                    t = 4 * p + k
                    x_w[t] = stt(X[:, t, :], b[:, k * 128:(k + 1) * 128], RR[:, 3, k, hh:hh + 1], X[:, t, :],
                                 ALU.mult, ALU.add, d, r_r, x_w[t])
                PS.give(b, x_w[t])
            f["ot", sl] = d
            f["rr"] = x_w[4 * p + 3]

        def run(*gens):
            gens = list(gens)
            while gens:
                for g in list(gens):
                    try:
                        next(g)
                    except StopIteration:
                        gens.remove(g)

        for p in range(NP):
            run(prep(p))
            for g in range(0, NG, 2):
                run(group(p, g, 0), group(p, g + 1, 1))

        last = f["rr"]
        KQf = KQ[:, :, :, :, :].rearrange("p a b c d -> p (a b c d)")
        AMf = AMt[:, :, :, :, :].rearrange("p a b c d -> p (a b c d)")
        free_kq, free_am, free_w = f["kq", 7], f["ot", 1], f["ot", 1]
        wg = KQf[:, 0:4096].rearrange("p (e f) -> p e f", e=NE)
        wu = KQf[:, 4096:8192].rearrange("p (e f) -> p e f", e=NE)
        wd = AMf[:, 0:4096].rearrange("p (e f d) -> p e f d", e=NE, f=4)
        sgn = WQ[:, 0:128]
        awq = WQ[:, 128:640].rearrange("p (m g c) -> p m g c", m=4, g=4)
        awk = WQ[:, 640:768].rearrange("p (g c) -> p g c", g=4)
        awv = WQ[:, 768:800]
        awo = WQ[:, 800:928]
        wr = WQ[:, 928:936]
        tri = WQ[:, 936:1064].rearrange("p (t a b) -> p t a b", t=2, a=8)
        amask = WQ[:, 1088:1600].bitcast(BF16).rearrange("p (o n) -> p o n", o=2)
        Xf = WQ[:, 1600:2112]
        z_aq = fill(WQ[:, 128:768], 0.0, free_w)
        l_wg = load(wg, wg_d, free_kq)
        l_wu = load(wu, wu_d, free_kq)
        l_wd = load(wd, wd_d, free_am)
        l_sg = load(sgn, sgn_d, free_w)
        l_aq = load(awq.rearrange("p m g c -> p (m g) c")[:, :, 0:8], awq_d, z_aq)
        l_ak = load(awk[:, :, 0:8], awk_d, z_aq)
        l_av = load(awv, awv_d, free_w)
        l_ao = load(awo, awo_d, free_w)
        l_wr = load(wr, wr_d, free_w)
        l_tri = load(tri, tri_d, free_w)
        c_sg = act.put(lambda e: e.activation(sgn, sgn, ACT.Sign), (l_sg,))
        c_am = cp(amask[:, 0, :].rearrange("p (m s) -> p m s", m=4), emask[:, 128:256].unsqueeze(1).to_broadcast([128, 4, 128]),
                  free_w)
        bq, bqf = PS.take()
        d = tr(bq[:, 0:128], emask[:, 128:256], ident[:, :], *bqf)
        c_am2 = cp(amask[:, 1, 0:128], bq[:, 0:128], d)
        PS.give(bq, c_am2)

        def signed(p):
            d = norm([4 * p + k for k in range(4)], xn[:, :, :], f.get("xn"))
            x_r, f["xn"] = transposed(xn, xnT, 4, d, f.get("xnT"), f.get("xnT2"))
            b, fr = PS.take()
            for k in range(4):
                d = mm(b[:, k * 128:(k + 1) * 128], xnT[:, k * 128:(k + 1) * 128], sgn, x_r, c_sg, *fr)
            f["xnT"] = d
            d = tt(X[:, 4 * p:4 * p + 4, :], X[:, 4 * p:4 * p + 4, :], b[:, :].rearrange("p (t n) -> p t n", t=4),
                   ALU.add, d)
            PS.give(b, d)
            for k in range(4):
                x_w[4 * p + k] = d
            yield

        BT = sb("BT", [128, 1])
        YFf = YFt[:, :, :, :].rearrange("p a b c -> p (a b c)")
        Vf = Vt[:, :, :, :, :].rearrange("p a b c d -> p (a b c d)")
        Uf = Ut[:, :, :, :, :].rearrange("p a b c d -> p (a b c d)")
        YPf = YPt[:, :, :, :].rearrange("p a b c -> p (a b c)")
        QT = YFf[:, 0:1024].rearrange("p (m t) -> p m t", m=4)
        KT = YFf[:, 1024:1280]
        V9 = YFf[:, 1280:1352].rearrange("p (c g d) -> p c g d", c=2, g=4)
        MX = YFf[:, 1360:1392].rearrange("p (c m g) -> p c m g", c=2, m=4)
        MXP = YFf[:, 1536:1536 + 256].rearrange("p (c x) -> p c x", c=2)
        CT = YPf[:, 0:256].rearrange("p (c n) -> p c n", c=2)
        CTT = YPf[:, 256:512]
        RC = YPf[:, 512:544].rearrange("p (c h) -> p c h", c=2)
        PT = Bufs([Vf[:, i * 512:(i + 1) * 512] for i in range(4)] + [Uf[:, i * 512:(i + 1) * 512] for i in range(4)])
        z_m = fill(YFf[:, 1536:1792], 0.0, last)
        z_k = fill(YFf[:, 1280:1352], 1.0, last)

        def attend(b8):
            d = norm([2 * b8, 2 * b8 + 1], xn[:, :, :], f.get("xn"))
            x_r, f["xn"] = transposed(xn, xnT, 2, d, f.get("xnT"))
            bk, fk = PS.take()
            dk = mm(bk[:, 0:256], awk.rearrange("p g c -> p (g c)"), xnT[:, 0:256], x_r, l_ak, z_aq, *fk)
            for c in range(2):
                dv = mm(bk[:, 256 + 32 * c:288 + 32 * c], xnT[:, c * 128:(c + 1) * 128], awv, l_av, x_r)
            bqs = []
            for m2 in range(2):
                bq, fq = PS.take()
                for m in range(2):
                    dq = mm(bq[:, m * 256:(m + 1) * 256], awq[:, 2 * m2 + m, :, :].rearrange("p g c -> p (g c)"),
                            xnT[:, 0:256], x_r, l_aq, z_aq, *fq)
                bqs.append((bq, dq))
            f["xnT"] = dq
            k_r = tt(KT, bk[:, 0:256], BTones, ALU.add, dv, f.get("kt"), c_bt)
            v_r = cp(V9[:, :, :, 0:8], bk[:, 256:320].rearrange("p (c g d) -> p c g d", c=2, g=4), dv, z_k, f.get("v9"))
            PS.give(bk, v_r)
            for m2, (bq, dq) in enumerate(bqs):
                q_r = ac(QT[:, 2 * m2:2 * m2 + 2, :], bq[:, :].rearrange("p (m t) -> p m t", m=2), ACT.Copy, dq, f.get("qt"))
                PS.give(bq, q_r)
            yield
            for c in range(2):
                n = 128 * (c + 1)
                per = 512 // n
                for g in range(4):
                    for m0 in range(0, 4, per):
                        b, fr = PS.take()
                        for m in range(m0, m0 + per):
                            o = (m - m0) * n
                            mm(b[:, o:o + n], QT[32 * g:32 * g + 8, m, c * 128:(c + 1) * 128], KT[32 * g:32 * g + 8, 0:n],
                               k_r, q_r, *fr, start=m == m0, stop=False, shared=True)
                            d = mm(b[:, o + n - 128:o + n], identb[:, :], amask[:, 1, 0:128], c_am2,
                                   start=False, stop=True, shared=True)
                        mx_r = red(MX[:, c, m0:m0 + per, g], b[:, :].rearrange("p (m t) -> p m t", m=per), ALU.max, d,
                                   f.get("mx"))
                        PS.give(b, mx_r)
                    yield
            for m in range(4):
                for c in range(2):
                    d = ts(MXP[:, c, :].rearrange("p (g x) -> p g x", g=4)[:, :, 8], MX[:, c, m, :], -1.0, None,
                           ALU.mult, None, mx_r, z_m, f.get("mxp"))
                b, fr = PS.take()
                for c in range(2):
                    d = tr(b[:, c * 128:(c + 1) * 128], MXP[:, c, :], ident[:, :], d, *fr)
                f["mxp"] = d
                q_r = tt(QT[:, m, :], QT[:, m, :], b[:, 0:256], ALU.add, d)
                PS.give(b, q_r)
            f["mx"] = d
            yield
            for g in range(4):
                pts = {}
                for c in range(2):
                    for t in range(c + 1):
                        b, fr = PS.take()
                        b3 = b[:, :].rearrange("p (m s) -> p m s", m=4)
                        d = mm(b3, KT[32 * g:32 * g + 9, t * 128:(t + 1) * 128], QT[32 * g:32 * g + 9, :, c * 128:(c + 1) * 128],
                               k_r, q_r, *fr, start=True, stop=t != c, shared=True)
                        if t == c:
                            d = mm(b[:, :], identb[:, :], amask[:, 0, :], c_am, start=False, stop=True, shared=True)
                        pt, pfr = PT.take()
                        r = ac(pt, b[:, :], ACT.Exp, d, *pfr, scale=8.0 ** -0.5)
                        PS.give(b, r)
                        pts[c, t] = (pt, r)
                b, fr = PS.take()
                for c in range(2):
                    for m in range(4):
                        o = (c * 4 + m) * 9
                        for t in range(c + 1):
                            pt, r = pts[c, t]
                            d = mm(b[:, o:o + 9], pt[:, m * 128:(m + 1) * 128], V9[:, t, g, :], r, v_r, *fr,
                                   start=t == 0, stop=t == c)
                for c in range(2):
                    for t in range(c + 1):
                        PT.give(pts[c, t][0], d)
                b4 = b[:, 0:72].rearrange("p (c m d) -> p c m d", c=2, m=4)
                r = dve.put(lambda e, o=RC[:, :, 4 * g:4 * g + 4], a=b4[:, :, :, 8]: e.reciprocal(o, a), (d, f.get("rc")))
                for c in range(2):
                    r2 = tt(CT[:, c, 32 * g:32 * g + 32].rearrange("p (m d) -> p m d", m=4), b4[:, c, :, 0:8],
                            RC[:, c, 4 * g:4 * g + 4].unsqueeze(2).to_broadcast([128, 4, 8]), ALU.mult, r, f.get("ct"))
                PS.give(b, r2)
                f["rc"] = r2
                yield
            f["kt"] = f["qt"] = f["v9"] = d
            r, f["ct"] = transposed(CT, CTT, 2, r2, f.get("ctt"))
            b, fr = PS.take()
            for c in range(2):
                d = mm(b[:, c * 128:(c + 1) * 128], CTT[:, c * 128:(c + 1) * 128], awo, r, l_ao, *fr)
            f["ctt"] = d
            d = tt(X[:, 2 * b8:2 * b8 + 2, :], X[:, 2 * b8:2 * b8 + 2, :], b[:, 0:256].rearrange("p (t n) -> p t n", t=2),
                   ALU.add, d)
            PS.give(b, d)
            x_w[2 * b8] = x_w[2 * b8 + 1] = d
            yield

        BTi = sb("BTi", [128, 1])
        c_bt0 = red(BTi[:, 0:1], ident[:, 8:128:32], ALU.add, l_id)
        c_bt = c_bt0
        BTones = BTi[:, 0:1].to_broadcast([128, 256])

        LG = sb("LG", [128, 4, 8])
        SC = sb("SC", [128, 4, 8])
        S1 = sb("S1", [128, 4])
        CB = sb("CB", [128, 4, 8])
        CMP = YPf[:, 0:256].rearrange("p (t a b) -> p t a b", t=4, a=8)
        CM2 = YPf[:, 256:512].rearrange("p (t a b) -> p t a b", t=4, a=8)
        RG = Bufs([ETt[:, i, :] for i in range(3)])
        HB = Bufs([YFf[:, i * 512:(i + 1) * 512] for i in range(4)] + [Vf[:, i * 512:(i + 1) * 512] for i in range(4)])

        def experts(p):
            d = norm([4 * p + k for k in range(4)], xn[:, :, :], f.get("xn"))
            x_r, f["xn"] = transposed(xn, xnT, 4, d, f.get("xnT"))
            b, fr = PS.take()
            for k in range(4):
                d = mm(b[:, k * 8:k * 8 + 8], xnT[:, k * 128:(k + 1) * 128], wr, x_r, l_wr, *fr)
            r = cp(LG[:, :, :], b[:, 0:32].rearrange("p (t e) -> p t e", t=4), d)
            PS.give(b, r)
            d = red(S1[:, :], LG[:, :, :], ALU.max, r)
            d = tt(LG[:, :, :], LG[:, :, :], S1[:, :].unsqueeze(2).to_broadcast([128, 4, 8]), ALU.subtract, d)
            d = ac(SC[:, :, :], LG[:, :, :], ACT.Exp, d)
            d = red(S1[:, :], SC[:, :, :], ALU.add, d)
            d = dve.put(lambda e: e.reciprocal(S1[:, :], S1[:, :]), (d,))
            d_s = tt(SC[:, :, :], SC[:, :, :], S1[:, :].unsqueeze(2).to_broadcast([128, 4, 8]), ALU.mult, d)
            other = SC[:, :, :].unsqueeze(2).to_broadcast([128, 4, 8, 8])
            own = SC[:, :, :].unsqueeze(3).to_broadcast([128, 4, 8, 8])
            for t in range(4):
                d1 = tt(CMP[:, t], other[:, t], own[:, t], ALU.is_ge, d_s)
                d2 = tt(CM2[:, t], other[:, t], own[:, t], ALU.is_gt, d_s)
            for t in range(4):
                d = tt(CMP[:, t], CMP[:, t], tri[:, 0], ALU.mult, d1, l_tri)
                d2 = tt(CM2[:, t], CM2[:, t], tri[:, 1], ALU.mult, d2)
            d = tt(CMP, CMP, CM2, ALU.add, d2)
            d = red(CB[:, :, :], CMP, ALU.add, d)
            d = stt(CB[:, :, :], CB[:, :, :], 1.5, SC[:, :, :], ALU.is_lt, ALU.mult, d)
            d = red(S1[:, :], CB[:, :, :], ALU.add, d)
            d = ts(S1[:, :], S1[:, :], 1.1920928955078125e-07, None, ALU.add, None, d)
            d = dve.put(lambda e: e.reciprocal(S1[:, :], S1[:, :]), (d,))
            cb_r = tt(CB[:, :, :], CB[:, :, :], S1[:, :].unsqueeze(2).to_broadcast([128, 4, 8]), ALU.mult, d)

            def down(ex, hbs):
                b, fr = PS.take()
                for k in range(4):
                    for j in range(4):
                        d = mm(b[:, k * 128:(k + 1) * 128], hbs[j][0][:, k * 128:(k + 1) * 128], wd[:, ex, j, :],
                               hbs[j][1], l_wd, *fr, start=j == 0, stop=j == 3)
                for j in range(4):
                    HB.give(hbs[j][0], d)
                for k in range(4):
                    t = 4 * p + k
                    x_w[t] = stt(X[:, t, :], b[:, k * 128:(k + 1) * 128], CB[:, k, ex:ex + 1], X[:, t, :],
                                 ALU.mult, ALU.add, d, cb_r, x_w[t])
                PS.give(b, x_w[t])

            prev = None
            for ex in range(NE):
                hbs = []
                for j in range(4):
                    bg, fg = PS.take()
                    bu, fu = PS.take()
                    dg = mm(bg[:, :], wg[:, ex, j * 128:(j + 1) * 128], xnT[:, :], x_r, l_wg, *fg)
                    du = mm(bu[:, :], wu[:, ex, j * 128:(j + 1) * 128], xnT[:, :], l_wu, *fu)
                    rg, rfr = RG.take()
                    r = ac(rg, bg[:, :], ACT.Relu, dg, *rfr)
                    PS.give(bg, r)
                    hb, hfr = HB.take()
                    d = tt(hb, bu[:, :], rg, ALU.mult, du, r, *hfr)
                    PS.give(bu, d)
                    RG.give(rg, d)
                    hbs.append((hb, d))
                if prev:
                    down(ex - 1, prev)
                prev = hbs
                yield
            f["xnT"] = du
            down(NE - 1, prev)
            for k in range(4):
                t = 4 * p + k
                count["out"] += 16
                sp.put(lambda e, o=out_d[t // 2, (t % 2) * 128:(t % 2) * 128 + 128, :], a=X[:, t, :]: e.dma_start(o, a),
                       (x_w[t],), s_out, count["out"])
            yield

        for p in range(NP):
            run(signed(p))
        for b8 in range(NB):
            run(attend(b8))
        ld = f["qt"]
        for p in range(NP):
            run(experts(p))

        for q in (pe, act, dve, pool, sp):
            q.number()
        block = ctx.enter_context(nc.Block())

        @block.tensor
        def _(e):
            pe.emit(e)

        @block.scalar
        def _(e):
            act.emit(e)

        @block.vector
        def _(e):
            dve.emit(e)

        @block.gpsimd
        def _(e):
            pool.emit(e)

        @block.sync
        def _(e):
            sp.emit(e)
            e.wait_ge(s_out, count["out"])


def kernel(**inputs):
    import numpy as np
    import concourse.bacc as _bacc
    from concourse import mybir as _mybir
    from concourse.bass_utils import run_bass_kernel_spmd as _run

    i = {k: np.asarray(v) for k, v in inputs.items()}
    c = np.ascontiguousarray
    f4 = np.float32
    r = np.arange(128)
    arrays = {
        "x": i["L0_attn_x"],
        "wqkv": np.concatenate([i["L0_attn_Wq"].T, i["L0_attn_Wk"].T, i["L0_attn_Wv"].T], axis=1),
        "conv": np.concatenate([i["L0_attn_conv_q"], i["L0_attn_conv_k"], i["L0_attn_conv_v"]]).reshape(32, 128, 4).transpose(1, 0, 2),
        "wab": np.concatenate([i["L0_attn_Wa"].T, i["L0_attn_Wb"].T], axis=1),
        "gate": np.stack([i["L0_attn_A_log"], i["L0_attn_dt_bias"]], axis=1),
        "wo": i["L0_attn_Wo"].T.reshape(16, 128, 128).transpose(1, 0, 2),
        "sgn": i["L0_ffn_weight"].T,
        "awq": i["L1_attn_wq"].T.reshape(128, 4, 4, 8).transpose(0, 2, 1, 3).reshape(128, 16, 8),
        "awk": i["L1_attn_wk"].T.reshape(128, 4, 8),
        "awv": i["L1_attn_wv"].T,
        "awo": i["L1_attn_wo"].T,
        "wr": i["L1_ffn_Wr"].T,
        "wg": i["L1_ffn_Wg"].transpose(2, 0, 1),
        "wu": i["L1_ffn_Wu"].transpose(2, 0, 1),
        "wd": i["L1_ffn_Wd"].transpose(2, 0, 1).reshape(4, 128, 8, 128).transpose(1, 2, 0, 3),
    }
    s, t = r[:, None], r[None, :]
    lm = np.zeros((128, 6, 64), f4)
    for lv in range(6):
        m = 1 << lv
        a, b = (s % 64) // m, t[:, :64] // m
        lm[:, lv, :] = (a % 2 == 1) & (b == a - 1)
    lm[:, 0, :] = (s % 2 == 0) & (t[:, :64] == s % 64 + 1)
    sel = np.zeros((128, 8, 16), f4)
    for k in range(8):
        sel[:, k, :] = np.arange(16)[None, :] == 2 * k + s // 64
    reset = np.ones((16, 512), f4)
    reset[:, ::256] = 0
    e = np.arange(8)
    tri = np.stack([e[None, :] < e[:, None], e[None, :] > e[:, None]]).astype(f4)
    arrays |= {
        "ident": np.eye(128, dtype=f4),
        "idp": (s % 64 == t[:, :64]).astype(f4),
        "emask": np.concatenate([np.where(t <= s, f4(-1e30), f4(0)), np.where(t < s, f4(-1e30), f4(0))], axis=1),
        "lmask": lm,
        "sel": sel,
        "reset": reset,
        "tri": np.broadcast_to(tri, (128, 2, 8, 8)),
    }
    nc = _bacc.Bacc("TRN2", target_bir_lowering=False, num_devices=1)
    arrays = {f"in_{k}_dram": c(v) for k, v in arrays.items()}
    args = [nc.dram_tensor(k, v.shape, _mybir.dt.from_np(v.dtype), kind="ExternalInput").ap() for k, v in arrays.items()]
    out = nc.dram_tensor("out_0_dram", (NB, T, D), _mybir.dt.float32, kind="ExternalOutput").ap()
    program(nc, *args, out)
    res = _run(nc, [arrays], core_ids=[0])
    return res.results[0]["out_0_dram"]
```

```python
import concourse.bass as bass
from concourse import mybir
from contextlib import ExitStack

F32 = mybir.dt.float32
BF16 = mybir.dt.bfloat16
ALU = mybir.AluOpType
ACT = mybir.ActivationFunctionType
AX = mybir.AxisListType

NB, T, D = 8, 256, 128
H, DK, DV = 16, 64, 128
NE, DFF = 8, 512
NP = NB // 2
NT = 16
GH = 2
NG = H // GH
NJ = GH * 4
NS = 3
NTB = 7
LAG = 9


class Done:

    def __init__(self):
        self.used = False
        self.sem = None
        self.value = 0


class Queue:

    def __init__(self, sem):
        self.sem = sem
        self.items = []
        self.chained = False

    def put(self, fn, waits, dma_sem=None, count=0):
        if self.chained and self.items:
            waits = (*waits, self.items[-1][2])
        for w in waits:
            if w is not None:
                w.used = True
        d = Done()
        if dma_sem is not None:
            d.sem, d.value = dma_sem, count
        self.items.append((fn, waits, d, 1 if dma_sem is None else 16))
        return d

    def number(self):
        n = 0
        for _, _, d, step in self.items:
            if step == 1 and d.used:
                n += 1
                d.sem, d.value = self.sem, n

    def emit(self, eng):
        seen = {}
        for fn, waits, d, step in self.items:
            for w in waits:
                if w is not None and seen.get(id(w.sem), 0) < w.value:
                    eng.wait_ge(w.sem, w.value)
                    seen[id(w.sem)] = w.value
            ins = fn(eng)
            if step == 16 or d.used:
                ins.then_inc(d.sem, step)


class Bufs:

    def __init__(self, bufs):
        self.free = [(b, ()) for b in bufs]

    def take(self):
        return self.free.pop(0)

    def give(self, b, *dones):
        self.free.append((b, dones))


def program(nc, x_d, wqkv_d, conv_d, wab_d, gate_d, wo_d, sgn_d, awq_d, awk_d, awv_d, awo_d,
            wr_d, wg_d, wu_d, wd_d, ident_d, idp_d, emask_d, lmask_d, sel_d, reset_d, tri_d, out_d):
    with ExitStack() as ctx:
        def sb(name, shape, dt=F32):
            return ctx.enter_context(nc.sbuf_tensor(name, shape, dt))

        def sem(name):
            return ctx.enter_context(nc.semaphore(name))

        pe, act, dve, pool, sp = (Queue(sem(f"s_{n}")) for n in ("pe", "act", "dve", "pool", "sp"))

        pool.chained = True

        def mm(out, l, r, *waits, start=True, stop=True, shared=False):
            return pe.put(lambda e: e.matmul(out, l, r, start=start, stop=stop, skip_group_check=shared), waits)

        def tr(out, a, i, *waits):
            return pe.put(lambda e: e.transpose(out, a, i), waits)

        def ac(out, a, f, *waits, scale=1.0, bias=0.0):
            return act.put(lambda e: e.activation(out, a, f, scale=scale, bias=bias), waits)

        def tt(out, a, b, op, *waits, q=dve):
            return q.put(lambda e: e.tensor_tensor(out, a, b, op), waits)

        def ts(out, a, s1, s2, op0, op1, *waits):
            if op1 is None:
                return dve.put(lambda e: e.tensor_scalar(out, a, s1, None, op0), waits)
            return dve.put(lambda e: e.tensor_scalar(out, a, s1, s2, op0, op1), waits)

        def stt(out, a, s, b, op0, op1, *waits):
            return dve.put(lambda e: e.scalar_tensor_tensor(out, a, s, b, op0, op1), waits)

        def cp(out, a, *waits, q=dve):
            return q.put(lambda e: e.tensor_copy(out, a), waits)

        def fill(out, v, *waits, q=dve):
            return q.put(lambda e: e.memset(out, v), waits)

        def vtr(out, a, *waits):
            return dve.put(lambda e: e.transpose(out, a), waits)

        def red(out, a, op, *waits):
            return dve.put(lambda e: e.tensor_reduce(out, a, AX.X, op), waits)

        nload = [0]

        def load(dst, src, *waits):
            nload[0] += 1
            return sp.put(lambda e: e.dma_start(dst, src), waits, sem(f"s_ld{nload[0]}"), 16)

        s_rows, s_out = [sem(f"s_rows{i}") for i in range(NS)], sem("s_out")
        count = {0: 0, 1: 0, 2: 0, "out": 0}

        banks = [ctx.enter_context(nc.psum_tensor(f"bank{i}", [128, 512], F32)) for i in range(8)]
        PS = Bufs(banks)

        X = sb("X", [128, NT, 128])
        ident = sb("ident", [128, 128])
        identb = sb("identb", [128, 128], BF16)
        idp = sb("idp", [128, 1, 64])
        emask = sb("emask", [128, 256])
        emaskb = sb("emaskb", [128, 2, 128], BF16)
        lmask = sb("lmask", [128, 6, 64])
        sel = sb("sel", [128, 8, 16])
        wab = sb("wab", [128, 32])
        cst = sb("cst", [128, 2])
        nh = sb("nh", [128, 8])
        conv = sb("conv", [128, 32, 4])
        WQ = sb("WQ", [128, 6144])
        wqkv = WQ[:, 0:4096]
        wo = WQ[:, 4096:6144].rearrange("p (h d) -> p h d", h=H)

        l_x = load(X[:, :, :], x_d.rearrange("b (c p) d -> p (b c) d", p=128))
        l_id = load(ident[:, :], ident_d)
        l_wq = load(wqkv, wqkv_d)
        l_cv = load(conv[:, :, :], conv_d)
        l_wab = load(wab[:, :], wab_d)
        SM = sb("SM", [128, 5896])
        gt = SM[32:48, 0:3072].rearrange("p (k t) -> p k t", k=6)
        spl = SM[32:48, 3072:5376].bitcast(BF16).rearrange("p (k t) -> p k t", k=9)
        reset = SM[32:48, 5376:5888]
        gate = SM[32:48, 5888:5892]
        CRt = SM[0:6, 0:1536].bitcast(BF16).rearrange("p (s h t) -> p s h t", s=3, h=GH)
        DRt = SM[0:6, 1536:4608].bitcast(BF16).rearrange("p (s h b k t) -> p s h b k t", s=3, h=GH, b=2, k=2)
        l_gate = load(gate[:, 0:2], gate_d)
        l_sel = load(sel[:, :, :], sel_d)
        l_em = load(emask[:, :], emask_d)
        l_idp = load(idp[:, 0, :], idp_d)
        l_lm = load(lmask[:, :, :], lmask_d)
        l_rs = load(reset, reset_d)
        l_wo = load(wo, wo_d)

        c_idb = cp(identb[:, :], ident[:, :], l_id)
        c_emb = cp(emaskb[:, :, :], emask[:, :].rearrange("p (k t) -> p k t", k=2), l_em)
        c_cv = ts(conv[:, :, :], conv[:, :, :], 0.5, None, ALU.mult, None, l_cv)
        c_half = fill(nh[:, :], -0.5)
        c_one = fill(cst[:, 0:1], 1.0)
        g_e = ac(gate[:, 2:3], gate[:, 0:1], ACT.Exp, l_gate)
        g_n = ts(gate[:, 3:4], gate[:, 2:3], -1.0, None, ALU.mult, None, g_e)

        KQ = sb("KQ", [128, 8, 2, 2, 256])
        AMt = sb("AM", [128, NS, GH, 2, 768])
        YFt = sb("YF", [128, NS, NJ, 128])
        YPt = sb("YP", [128, NS, NJ, 64])
        XPt = sb("XP", [128, NS, NJ, 64])
        PPt = sb("PP", [128, NS, NJ, 64])
        Vt = sb("V", [128, NS, GH, 4, 128])
        Ut = sb("U", [128, NS, GH, 4, 128])
        OTb = Vt[:, :, :, :, :].rearrange("p s h t n -> p s h (t n)")
        yp_t = sb("yp_t", [128, 2, 2, 259])
        tb_t = sb("tb_t", [128, NTB, 512])
        xT_t = sb("xnT", [128, 2, 512])
        st_t = sb("st", [128, 3, 40])
        TB = Bufs([tb_t[:, i, :] for i in range(NTB)])
        XT = Bufs([xT_t[:, i, :] for i in range(2)])
        ST = Bufs([st_t[:, i, :] for i in range(3)])
        LQt = sb("LQ", [128, 2, 4, H])
        E2t = sb("E2", [128, 2, 4, H])
        RRt = sb("RR", [128, 3, 4, 4, GH])

        YPAD = Bufs([yp_t[:, i, :, :] for i in range(2)])

        z_pad = fill(yp_t[:, :, :, 0:3], 0.0)
        z_yf = fill(YFt[:, :, :, :], 0.0)
        z_cr = fill(CRt[:, :, :, :], 1.0)
        z_dr = fill(DRt[:, :, :, :, :, :], 1.0)

        f = {}
        x_w = [l_x] * NT

        def grab(pool, n=1):
            while len(pool.free) < n:
                yield
            return pool.take() if n == 1 else [pool.take() for _ in range(n)]

        def normed(tiles):
            n = len(tiles)
            st, sfr = yield from grab(ST)
            st6, mv, rs = (st[:, o:o + w * 4].rearrange("p (k w) -> p k w", k=4) for o, w in ((0, 6), (24, 2), (32, 2)))
            for k, t in enumerate(tiles):
                d = dve.put(lambda e, o=st6[:, k, :], a=X[:, t, :]: e.bn_stats(o, a), (x_w[t], *sfr))
            for k in range(n):
                d2 = dve.put(lambda e, o=mv[:, k, :], a=st6[:, k, :]: e.bn_aggr(o, a), (d,))
            d = ts(rs[:, 0:n, 0], mv[:, 0:n, 1], 1e-5, None, ALU.add, None, d2)
            d = tt(rs[:, 0:n, 0], rs[:, 0:n, 0], nh[:, 0:n], ALU.pow, d, c_half, q=pool)
            yield
            xb, nfr = yield from grab(TB)
            xn = xb.rearrange("p (k n) -> p k n", k=4)
            for k, t in enumerate(tiles):
                d2 = ts(xn[:, k, :], X[:, t, :], mv[:, k, 0:1], rs[:, k, 0:1], ALU.subtract, ALU.mult, d, *nfr)
            ST.give(st, d2)
            xT, tfr = yield from grab(XT)
            yield
            b, fr = yield from grab(PS)
            for k in range(n):
                d = tr(b[:, k * 128:(k + 1) * 128], xn[:, k, :], ident[:, :], d2, l_id, *fr)
            TB.give(xb, d)
            yield
            r = ac(xT[:, 0:n * 128], b[:, 0:n * 128], ACT.Copy, d, *tfr)
            PS.give(b, r)
            return xT, r

        def transposed(src, dst, n, ready, *free):
            b, fr = yield from grab(PS)
            for k in range(n):
                d = tr(b[:, k * 128:(k + 1) * 128], src[:, k, :], ident[:, :], ready, l_id, *fr)
            yield
            r = ac(dst[:, 0:n * 128], b[:, 0:n * 128], ACT.Copy, d, *free)
            PS.give(b, r)
            return r, d

        def silu_tile(ct, dst, xT, x_r, *free):
            b, fr = yield from grab(PS)
            m = mm(b[:, :], wqkv[:, ct * 128:(ct + 1) * 128], xT, x_r, l_wq, *fr)
            y, yfr = yield from grab(YPAD)
            yield
            r = ac(y[:, :, 3:259], b[:, :].rearrange("p (b t) -> p b t", b=2), ACT.Copy, m, z_pad, *yfr)
            PS.give(b, r)
            c, cfr = yield from grab(TB)
            yield
            c2 = c.rearrange("p (b t) -> p b t", b=2)
            d = ts(c2, y[:, :, 0:256], conv[:, ct, 0:1], None, ALU.mult, None, r, c_cv, *cfr)
            for j in range(1, 4):
                d = stt(c2, y[:, :, j:j + 256], conv[:, ct, j:j + 1], c2, ALU.mult, ALU.add, d)
            yield
            t = y[:, :, 3:259]
            r = ac(t, c2, ACT.Tanh, d)
            yield
            o = c2 if dst is None else dst
            d = stt(o, t, 1.0, c2, ALU.add, ALU.mult, r, *free)
            YPAD.give(y, d)
            if dst is None:
                return d, m, c
            TB.give(c, d)
            return d, m

        ready = {}

        def prep(p):
            LQ, E2 = LQt[:, p % 2], E2t[:, p % 2]
            xT, x_r = yield from normed([4 * p + k for k in range(4)])
            ready["x", p] = xT, x_r
            yield
            nb_, nfr = yield from grab(PS)
            nk, nq = nb_[32:48, :], nb_[64:80, :]
            for i8 in range(8):
                while p and (p - 1, i8) not in gram_queued:
                    yield
                for kq, nbank in ((0, nk), (1, nq)):
                    d, _ = yield from silu_tile((1 - kq) * 8 + i8, KQ[:, i8, :, kq, :], xT, x_r, f.get(("kq", i8)))
                    ready["kq", p, i8] = d
                    q, qfr = yield from grab(TB)
                    yield
                    s = ac(q.rearrange("p (b t) -> p b t", b=2), KQ[:, i8, :, kq, :], ACT.Square, d, *qfr)
                    yield
                    dn = mm(nbank, sel[:, i8, :], q, s, l_sel, *nfr, start=i8 == 0, stop=i8 == 7)
                    TB.give(q, dn)
                    yield
            G = lambda k: gt[:, k, :]
            (ab, afr), (bb, bfr) = yield from grab(PS, 2)
            da = mm(ab[32:48, :], wab[:, 0:16], xT, l_wab, x_r, *afr)
            db = mm(bb[32:48, :], wab[:, 16:32], xT, l_wab, *bfr)
            yield
            d = ts(G(0), ab[32:48, :], gate[:, 1:2], None, ALU.add, None, da, g_n, f.get("spl"))
            PS.give(ab, d)
            d = ac(G(1), G(0), ACT.Abs, d)
            d = ac(G(1), G(1), ACT.Exp, d, scale=-1.0)
            d = ac(G(1), G(1), ACT.Ln, d, c_one, bias=cst[32:48, 0:1])
            yield
            d = stt(G(1), G(0), 0.0, G(1), ALU.max, ALU.add, d)
            d = ts(G(1), G(1), gate[:, 3:4], None, ALU.mult, None, d)
            d_g = dve.put(lambda e: e.tensor_tensor_scan(G(2), reset, G(1), 0.0, ALU.mult, ALU.add), (d, l_rs))
            d = ac(G(3), bb[32:48, :], ACT.Abs, db)
            d = ac(G(3), G(3), ACT.Exp, d, scale=-1.0)
            d = ac(G(3), G(3), ACT.Ln, d, bias=cst[32:48, 0:1])
            d_b = stt(G(3), bb[32:48, :], 0.0, G(3), ALU.min, ALU.subtract, d)
            PS.give(bb, d_b)
            yield
            d1 = ts(G(4), nk, 1e-12, None, ALU.max, None, dn, f.get("spl"))
            d2 = ts(G(5), nq, 1e-12, None, ALU.max, None, dn, f.get("lqT"))
            PS.give(nb_, d2)
            d1 = ac(G(4), G(4), ACT.Ln, d1)
            d2 = ac(G(5), G(5), ACT.Ln, d2)
            dc = stt(G(0), G(4), -0.5, G(2), ALU.mult, ALU.subtract, d1, d_g)
            d = stt(G(1), G(4), -0.5, G(2), ALU.mult, ALU.add, d_g)
            dd = stt(G(1), G(3), 0.6931471805599453, G(1), ALU.add, ALU.add, d, d_b)
            lq_r = ts(G(5), G(5), -0.5, None, ALU.mult, None, d2)
            for k, (src, dn) in enumerate(((0, dc), (1, dd), (2, d_g))):
                d = cp(spl[:, 3 * k, :], G(src), dn, dd, *(f.get(("rows", i)) for i in range(NS)), q=pool)
                d = tt(G(3), G(src), spl[:, 3 * k, :], ALU.subtract, d, q=pool)
                d = cp(spl[:, 3 * k + 1, :], G(3), d, q=pool)
                d = tt(spl[:, 3 * k + 2, :], G(3), spl[:, 3 * k + 1, :], ALU.subtract, d, q=pool)
            f["spl"] = d
            ready["spl", p] = d
            yield
            lb, lfr = yield from grab(PS)
            for k in range(4):
                d = tr(lb[:, k * 16:(k + 1) * 16], G(5)[:, k * 128:(k + 1) * 128], ident[32:48, 32:48], lq_r, *lfr)
            f["lqT"] = d
            yield
            ac(LQ, lb[:, 0:64].rearrange("p (t h) -> p t h", t=4), ACT.Exp, d, *(f.get(("rr", i)) for i in range(NS)))
            d = ac(E2, lb[:, 0:64].rearrange("p (t h) -> p t h", t=4), ACT.Exp, scale=2.0)
            PS.give(lb, d)
            ready["e2", p] = d

        def rows(p, g, sl, CR, DR):
            hs = slice(g * GH, g * GH + GH)
            for k in range(3):
                for r in range(3):
                    if k == 0:
                        dst, src = CR[r:r + 1, :, :], spl[hs, r, :]
                    else:
                        dst = DR[3 + r:4 + r, :, :, k - 1, :]
                        src = spl[hs, 3 * k + r, :].rearrange("h (b t) -> h b t", b=2)
                    count[sl] += 16
                    d = sp.put(lambda e, dst=dst, src=src: e.dma_start(dst, src),
                               (ready["spl", p], z_cr, z_dr, f.get(("ex", sl)), f.get(("rows", sl))), s_rows[sl], count[sl])
            f["rows", sl] = d
            return d

        def group(p, g, sl):
            AM, YF, YP, XP, PP, V, U, OTt = (a[:, sl] for a in (AMt, YFt, YPt, XPt, PPt, Vt, Ut, OTb))
            xT, x_r = ready["x", p]
            LQ, E2 = LQt[:, p % 2], E2t[:, p % 2]
            CR, DR = CRt[:, sl], DRt[:, sl]
            rows_r = rows(p, g, sl, CR, DR)
            for hh in range(GH):
                d, lastm, vt = yield from silu_tile(16 + g * GH + hh, None, xT, x_r)
                yield
                b, fr = yield from grab(PS)
                for k in range(4):
                    d2 = tr(b[:, k * 128:(k + 1) * 128], vt[:, k * 128:(k + 1) * 128], ident[:, :], d, *fr)
                TB.give(vt, d2)
                yield
                v_r = ac(V[:, hh, :, :], b[:, :].rearrange("p (t n) -> p t n", t=4), ACT.Copy, d2, f.get(("u", sl)), f.get(("ot", sl)))
                PS.give(b, v_r)
                yield
            if g == NG - 1:
                XT.give(xT, lastm)
            for hh in range(GH):
                h = g * GH + hh
                i8, hp = h // 2, 64 * (h % 2)
                for part in range(3):
                    (eb, efr), (kb, kfr) = yield from grab(PS, 2)
                    spans = [(part, 0, 0, 512)] if part < 2 else [(0, 128, 0, 256), (1, 128, 256, 256)]
                    for n, (b, s0, o, w) in enumerate(spans):
                        e3 = eb[:, o:o + w].rearrange("p (k t) -> p k t", k=2)
                        k3 = kb[:, o:o + w].rearrange("p (k t) -> p k t", k=2)
                        mm(e3, CR[0:6, hh, b * 256 + s0:b * 256 + s0 + 128], DR[0:6, hh, b, :, s0:256],
                           rows_r, *efr, start=n == 0, stop=False, shared=True)
                        de = mm(e3[:, :, 0:128], identb[:, :], emaskb[:, :, :], c_emb, c_idb,
                                start=False, stop=True, shared=True)
                        dk = mm(k3, KQ[hp:hp + 64, i8, b, 0, s0:s0 + 128], KQ[hp:hp + 64, i8, b, :, s0:256],
                                ready["kq", p, i8], *kfr)
                    f["ex", sl] = de
                    if h % 2:
                        f["kq", i8] = dk
                    et, tfr = yield from grab(TB)
                    yield
                    r = ac(et, eb[:, :], ACT.Exp, de, *tfr)
                    PS.give(eb, r)
                    yield
                    if part < 2:
                        dst = AM[:, hh, part, :].rearrange("p (c n) -> p c n", c=3)[:, 0:3:2, :]
                    else:
                        dst = AM[:, hh, :, 256:512]
                    am_r = tt(dst, kb[:, :].rearrange("p (k t) -> p k t", k=2), et.rearrange("p (k t) -> p k t", k=2),
                              ALU.mult, dk, r, f.get(("am", sl)))
                    PS.give(kb, am_r)
                    TB.give(et, am_r)
                    yield
            gram_queued.add((p, g))
            N4 = AM.rearrange("p h b (c n) -> p (h b) c n", c=3)
            N = lambda j, q, a: N4[64 * q:64 * q + 64, j // 2, j % 2, a:a + 64]
            W = lambda b: b[:, :].rearrange("p (j n) -> p j n", j=NJ)
            mask = lambda lv, q=slice(0, 128): lmask[q, lv:lv + 1, :].to_broadcast([q.stop - q.start, NJ, 64])
            for q in range(2):
                pq = slice(64 * q, 64 * q + 64)
                d = tt(YP[pq].rearrange("p (m c) n -> p m c n", c=2), N4[pq, :, 0:2, 64 * q:64 * q + 64],
                       mask(0, pq).rearrange("p (m c) n -> p m c n", c=2), ALU.mult, am_r, l_lm, f.get(("yf", sl)),
                       f.get(("inv", sl)))
            y_r = tt(YP[:, :, :], idp[:, :, :].to_broadcast([128, NJ, 64]), YP[:, :, :], ALU.subtract, d, l_idp)
            x_i = vtr(XP[:, :, :], YP[:, :, :], y_r, f.get(("inv", sl)))
            yield
            pp_f = f.get(("inv", sl))
            for lv in range(1, 6):
                b, fr = yield from grab(PS)
                for j in range(NJ):
                    for q in range(2):
                        pq = slice(64 * q, 64 * q + 64)
                        d = mm(b[pq, j * 64:j * 64 + 64], N(j, q, 64 * q), XP[pq, j, :], x_i, am_r, *fr)
                yield
                r = tt(PP[:, :, :], W(b), mask(lv), ALU.mult, d, pp_f)
                PS.give(b, r)
                yield
                if lv < 5:
                    b, fr = yield from grab(PS)
                else:
                    (b, fr), (b2, fr2) = yield from grab(PS, 2)
                for j in range(NJ):
                    for q in range(2):
                        pq = slice(64 * q, 64 * q + 64)
                        d = mm(b[pq, j * 64:j * 64 + 64], PP[pq, j, :], YP[pq, j, :], r, y_r, *fr)
                if lv == 5:
                    for j in range(NJ):
                        dx = mm(b2[0:64, j * 64:j * 64 + 64], YP[0:64, j, :], PP[0:64, j, :], *fr2)
                    d = dx
                pp_f = d
                yield
                y_r = tt(YP[:, :, :], YP[:, :, :], W(b), ALU.subtract, d)
                PS.give(b, y_r)
                if lv < 5:
                    x_i = vtr(XP[:, :, :], YP[:, :, :], y_r)
                else:
                    x_i = tt(XP[0:64], XP[0:64], W(b2)[0:64], ALU.subtract, dx)
                    PS.give(b2, x_i)
                yield
            b, fr = yield from grab(PS)
            for j in range(NJ):
                d = mm(b[64:128, j * 64:j * 64 + 64], N(j, 0, 64), XP[0:64, j, :], x_i, *fr)
            yield
            r = ts(PP[64:128], W(b)[64:128], -1.0, None, ALU.mult, None, d, pp_f)
            PS.give(b, r)
            r0 = cp(YF[0:64, :, 0:64], YP[0:64], y_r, z_yf, f.get(("yf", sl)), q=pool)
            r1 = cp(YF[64:128, :, 64:128], YP[64:128], y_r, z_yf, f.get(("yf", sl)), q=pool)
            yield
            b, fr = yield from grab(PS)
            for j in range(NJ):
                d = mm(b[0:64, j * 64:j * 64 + 64], PP[64:128, j, :], YP[64:128, j, :], r, y_r, *fr)
            f["inv", sl] = d
            yield
            r = ac(YF[0:64, :, 64:128], W(b)[0:64], ACT.Copy, d, z_yf, f.get(("yf", sl)))
            PS.give(b, r)
            yield

            def solve(c, *waits):
                b, fr = yield from grab(PS)
                for k in range(2 * GH):
                    d = mm(b[:, k * 128:(k + 1) * 128], YF[:, 2 * k + c, :], V[:, k // 2, 2 * (k % 2) + c, :], *waits, *fr)
                yield
                r = ac(U[:, :, c:4:2, :], b[:, :].rearrange("p (h b n) -> p h b n", h=GH, b=2), ACT.Copy, d, f.get(("o", sl)))
                PS.give(b, r)
                return r, d
            u1, _ = yield from solve(0, r, r0, r1, v_r)
            yield
            b, fr = yield from grab(PS)
            for k in range(2 * GH):
                d = mm(b[:, k * 128:(k + 1) * 128], AM[:, k // 2, k % 2, 128:256], U[:, k // 2, 2 * (k % 2), :], u1, *fr)
            yield
            r = tt(V[:, :, 1:4:2, :], V[:, :, 1:4:2, :], b[:, :].rearrange("p (h b n) -> p h b n", h=GH, b=2),
                   ALU.subtract, d)
            PS.give(b, r)
            yield
            u2, d = yield from solve(1, r)
            f["u", sl] = f["yf", sl] = d
            yield
            (sb_, sfr), b_ = yield from grab(PS, 2)
            o_r = []
            for hh in range(GH):
                b, fr = b_ if hh == 0 else (yield from grab(PS))
                for bt in range(2):
                    mm(b[:, bt * 256:bt * 256 + 256], U[:, hh, 2 * bt, :], AM[:, hh, bt, 512:768], u1, u2, *fr,
                       start=True, stop=False, shared=True)
                    d = mm(b[:, bt * 256 + 128:bt * 256 + 256], U[:, hh, 2 * bt + 1, :], AM[:, hh, bt, 384:512],
                           start=False, stop=True, shared=True)
                d_o = d
                q, qfr = yield from grab(TB)
                yield
                r = ac(q, b[:, :], ACT.Square, d, *qfr)
                r1 = ac(OTt[:, hh, :], b[:, :], ACT.Copy, f["u", sl])
                o_r.append(r1)
                PS.give(b, r1)
                yield
                for k in range(4):
                    d2 = mm(sb_[:, k * GH + hh:k * GH + hh + 1], q[:, k * 128:(k + 1) * 128], cst[:, 0:1], r, c_one, *sfr)
                TB.give(q, d2)
            f["am", sl] = f["o", sl] = d_o
            yield
            hs = slice(g * GH, g * GH + GH)
            RR = RRt[:, sl]
            A = lambda k: RR[:, k, :, :]
            d = tt(A(0), sb_[:, 0:4 * GH].rearrange("p (t h) -> p t h", t=4), E2[:, :, hs], ALU.mult,
                   d2, ready["e2", p], f.get(("rr", sl)))
            PS.give(sb_, d)
            d = ts(A(1), A(0), 1.0 / 128, 1e-6, ALU.mult, ALU.add, d)
            d = tt(A(2), A(1), nh[:, :].rearrange("p (t h) -> p t h", t=4), ALU.pow, d, c_half, q=pool)
            r_r = tt(A(3), A(2), LQ[:, :, hs], ALU.mult, d)
            yield
            for hh in range(GH):
                b, fr = yield from grab(PS)
                for k in range(4):
                    d = mm(b[:, k * 128:(k + 1) * 128], OTt[:, hh, k * 128:(k + 1) * 128], wo[:, g * GH + hh, :],
                           o_r[hh], l_wo, *fr)
                yield
                for k in range(4):
                    t = 4 * p + k
                    x_w[t] = stt(X[:, t, :], b[:, k * 128:(k + 1) * 128], RR[:, 3, k, hh:hh + 1], X[:, t, :],
                                 ALU.mult, ALU.add, d, r_r, x_w[t])
                PS.give(b, x_w[t])
            f["ot", sl] = d
            f["rr", sl] = x_w[4 * p + 3]

        def run(*gens):
            gens = list(gens)
            while gens:
                for g in list(gens):
                    try:
                        next(g)
                    except StopIteration:
                        gens.remove(g)

        gram_queued = set()
        run(prep(0))
        todo = [(p, g) for p in range(NP) for g in range(NG)]
        active, slots, since, cur = [], list(range(NS)), LAG, 0
        side = prep(1)
        while todo or active:
            if todo and slots and since >= LAG and (todo[0][0] == cur or side is None):
                p, g = todo.pop(0)
                if p != cur:
                    cur, side = p, prep(p + 1) if p + 1 < NP else None
                active.append((group(p, g, slots[0]), slots.pop(0)))
                since = 0
            since += 1
            for a in list(active):
                if next(a[0], "end") == "end":
                    active.remove(a)
                    slots.append(a[1])
            if side is not None and next(side, "end") == "end":
                side = None

        last = x_w[4 * NP - 1]
        KQf = KQ[:, :, :, :, :].rearrange("p a b c d -> p (a b c d)")
        AMf = AMt[:, :, :, :, :].rearrange("p a b c d -> p (a b c d)")
        free_kq, free_am, free_w = f["kq", 7], last, last
        wg = KQf[:, 0:4096].rearrange("p (e f) -> p e f", e=NE)
        wu = KQf[:, 4096:8192].rearrange("p (e f) -> p e f", e=NE)
        wd = AMf[:, 0:4096].rearrange("p (e f d) -> p e f d", e=NE, f=4)
        sgn = WQ[:, 0:128]
        awq = WQ[:, 128:640].rearrange("p (m g c) -> p m g c", m=4, g=4)
        awk = WQ[:, 640:768].rearrange("p (g c) -> p g c", g=4)
        awv = WQ[:, 768:800]
        awo = WQ[:, 800:928]
        wr = WQ[:, 928:936]
        tri = WQ[:, 936:1064].rearrange("p (t a b) -> p t a b", t=2, a=8)
        amask = WQ[:, 1088:1600].bitcast(BF16).rearrange("p (o n) -> p o n", o=2)
        Xf = WQ[:, 1600:2112]
        z_aq = fill(WQ[:, 128:768], 0.0, free_w)
        l_wg = load(wg, wg_d, free_kq)
        l_wu = load(wu, wu_d, free_kq)
        l_wd = load(wd, wd_d, free_am)
        l_sg = load(sgn, sgn_d, free_w)
        l_aq = load(awq.rearrange("p m g c -> p (m g) c")[:, :, 0:8], awq_d, z_aq)
        l_ak = load(awk[:, :, 0:8], awk_d, z_aq)
        l_av = load(awv, awv_d, free_w)
        l_ao = load(awo, awo_d, free_w)
        l_wr = load(wr, wr_d, free_w)
        l_tri = load(tri, tri_d, free_w)
        c_sg = act.put(lambda e: e.activation(sgn, sgn, ACT.Sign), (l_sg,))
        c_am = cp(amask[:, 0, :].rearrange("p (m s) -> p m s", m=4), emask[:, 128:256].unsqueeze(1).to_broadcast([128, 4, 128]),
                  free_w)
        bq, bqf = PS.take()
        d = tr(bq[:, 0:128], emask[:, 128:256], ident[:, :], *bqf)
        for k in range(4):
            c_am2 = cp(amask[:, 1, 128 * k:128 * k + 128], bq[:, 0:128], d)
        PS.give(bq, c_am2)

        def signed(p):
            xT, x_r = yield from normed([4 * p + k for k in range(4)])
            yield
            b, fr = yield from grab(PS)
            for k in range(4):
                d = mm(b[:, k * 128:(k + 1) * 128], xT[:, k * 128:(k + 1) * 128], sgn, x_r, c_sg, *fr)
            XT.give(xT, d)
            yield
            d = tt(X[:, 4 * p:4 * p + 4, :], X[:, 4 * p:4 * p + 4, :], b[:, :].rearrange("p (t n) -> p t n", t=4),
                   ALU.add, d)
            PS.give(b, d)
            for k in range(4):
                x_w[4 * p + k] = d
            yield

        flat = lambda a, n: a.rearrange("p " + " ".join("abcde"[:n]) + " -> p (" + " ".join("abcde"[:n]) + ")")
        YFf, YPf = flat(YFt[:, :, :, :], 3), flat(YPt[:, :, :, :], 3)
        XPf, PPf = flat(XPt[:, :, :, :], 3), flat(PPt[:, :, :, :], 3)
        Vf, Uf = flat(Vt[:, :, :, :, :], 4), flat(Ut[:, :, :, :, :], 4)
        PT = Bufs([a[:, i * 512:(i + 1) * 512] for a in (Vf, Uf) for i in range(6)])
        HB = Bufs([AMf[:, 4096 + i * 512:4608 + i * 512] for i in range(10)])
        for i in range(3):
            XT.give(PPf[:, i * 512:(i + 1) * 512], last)
        z_m = fill(XPf[:, 512:1024], 0.0, last)
        z_k = fill(YFf, 1.0, last)
        BT = sb("BT", [128, 1])
        c_bt = red(BT[:, 0:1], ident[:, 8:128:32], ALU.add, l_id)

        def attend(b8, sl):
            w = YFf[:, 1536 * sl:1536 * sl + 1536]
            QT = w[:, 0:1024].rearrange("p (m t) -> p m t", m=4)
            KT = w[:, 1024:1280]
            V9 = w[:, 1280:1352].rearrange("p (c g d) -> p c g d", c=2, g=4)
            MX = w[:, 1360:1392].rearrange("p (c m g) -> p c m g", c=2, m=4)
            MXP = XPf[:, 512 + 256 * sl:768 + 256 * sl].rearrange("p (c x) -> p c x", c=2)
            w = YPf[:, 768 * sl:768 * sl + 768]
            CT, CTT = w[:, 0:256].rearrange("p (c n) -> p c n", c=2), w[:, 256:512]
            RC = w[:, 512:544].rearrange("p (c h) -> p c h", c=2)
            F = lambda k: f.get((k, sl))
            xnT, x_r = yield from normed([2 * b8, 2 * b8 + 1])
            yield
            bk, fk = yield from grab(PS)
            dk = mm(bk[:, 0:256], awk.rearrange("p g c -> p (g c)"), xnT[:, 0:256], x_r, l_ak, z_aq, *fk)
            for c in range(2):
                dv = mm(bk[:, 256 + 32 * c:288 + 32 * c], xnT[:, c * 128:(c + 1) * 128], awv, l_av, x_r)
            yield
            k_r = tt(KT, bk[:, 0:256], BT[:, 0:1].to_broadcast([128, 256]), ALU.add, dv, F("ak"), c_bt, z_k)
            v_r = cp(V9[:, :, :, 0:8], bk[:, 256:320].rearrange("p (c g d) -> p c g d", c=2, g=4), dv, z_k, F("ak"))
            PS.give(bk, v_r)
            for m2 in range(2):
                bq, fq = yield from grab(PS)
                for m in range(2):
                    dq = mm(bq[:, m * 256:(m + 1) * 256], awq[:, 2 * m2 + m, :, :].rearrange("p g c -> p (g c)"),
                            xnT[:, 0:256], x_r, l_aq, z_aq, *fq)
                yield
                q_r = ac(QT[:, 2 * m2:2 * m2 + 2, :], bq[:, :].rearrange("p (m t) -> p m t", m=2), ACT.Copy, dq, z_k, F("ak"))
                PS.give(bq, q_r)
            XT.give(xnT, dq)
            yield
            for c in range(2):
                n = 128 * (c + 1)
                per = 512 // n
                for g in range(4):
                    for m0 in range(0, 4, per):
                        b, fr = yield from grab(PS)
                        for m in range(m0, m0 + per):
                            o = (m - m0) * n
                            mm(b[:, o:o + n], QT[32 * g:32 * g + 8, m, c * 128:(c + 1) * 128], KT[32 * g:32 * g + 8, 0:n],
                               k_r, q_r, *fr, start=m == m0, stop=False, shared=True)
                        tail_ = b[:, :].rearrange("p (m t) -> p m t", m=per)[:, :, n - 128:n]
                        d = mm(tail_, identb[:, :], amask[:, 1, 0:128 * per].rearrange("p (m t) -> p m t", m=per), c_am2,
                               start=False, stop=True, shared=True)
                        yield
                        mx_r = red(MX[:, c, m0:m0 + per, g], b[:, :].rearrange("p (m t) -> p m t", m=per), ALU.max, d,
                                   F("mx"), z_k)
                        PS.give(b, mx_r)
            yield
            for m in range(4):
                for c in range(2):
                    d = ts(MXP[:, c, :].rearrange("p (g x) -> p g x", g=4)[:, :, 8], MX[:, c, m, :], -1.0, None,
                           ALU.mult, None, mx_r, z_m, F("mxp"))
                yield
                b, fr = yield from grab(PS)
                for c in range(2):
                    dt = tr(b[:, c * 128:(c + 1) * 128], MXP[:, c, :], ident[:, :], d, *fr)
                f["mxp", sl] = dt
                yield
                q_r = tt(QT[:, m, :], QT[:, m, :], b[:, 0:256], ALU.add, dt, q_r)
                PS.give(b, q_r)
            f["mx", sl] = d
            yield
            for g in range(4):
                pts = {}
                for c in range(2):
                    for t in range(c + 1):
                        b, fr = yield from grab(PS)
                        b3 = b[:, :].rearrange("p (m s) -> p m s", m=4)
                        d = mm(b3, KT[32 * g:32 * g + 9, t * 128:(t + 1) * 128], QT[32 * g:32 * g + 9, :, c * 128:(c + 1) * 128],
                               k_r, q_r, *fr, start=True, stop=t != c, shared=True)
                        if t == c:
                            d = mm(b[:, :], identb[:, :], amask[:, 0, :], c_am, start=False, stop=True, shared=True)
                        yield
                        pt, pfr = yield from grab(PT)
                        r = ac(pt, b[:, :], ACT.Exp, d, *pfr, scale=8.0 ** -0.5)
                        PS.give(b, r)
                        pts[c, t] = (pt, r)
                yield
                b, fr = yield from grab(PS)
                for c in range(2):
                    for m in range(4):
                        o = (c * 4 + m) * 9
                        for t in range(c + 1):
                            pt, r = pts[c, t]
                            d = mm(b[:, o:o + 9], pt[:, m * 128:(m + 1) * 128], V9[:, t, g, :], r, v_r, *fr,
                                   start=t == 0, stop=t == c)
                for k in pts:
                    PT.give(pts[k][0], d)
                yield
                b4 = b[:, 0:72].rearrange("p (c m d) -> p c m d", c=2, m=4)
                r = dve.put(lambda e, o=RC[:, :, 4 * g:4 * g + 4], a=b4[:, :, :, 8]: e.reciprocal(o, a), (d, F("ct")))
                for c in range(2):
                    r2 = tt(CT[:, c, 32 * g:32 * g + 32].rearrange("p (m d) -> p m d", m=4), b4[:, c, :, 0:8],
                            RC[:, c, 4 * g:4 * g + 4].unsqueeze(2).to_broadcast([128, 4, 8]), ALU.mult, r, F("ct"))
                PS.give(b, r2)
            f["ak", sl] = d
            yield
            r, f["ct", sl] = yield from transposed(CT, CTT, 2, r2, F("ctt"))
            yield
            b, fr = yield from grab(PS)
            for c in range(2):
                d = mm(b[:, c * 128:(c + 1) * 128], CTT[:, c * 128:(c + 1) * 128], awo, r, l_ao, *fr)
            f["ctt", sl] = d
            yield
            d = tt(X[:, 2 * b8:2 * b8 + 2, :], X[:, 2 * b8:2 * b8 + 2, :], b[:, 0:256].rearrange("p (t n) -> p t n", t=2),
                   ALU.add, d)
            PS.give(b, d)
            x_w[2 * b8] = x_w[2 * b8 + 1] = d

        LG = sb("LG", [128, 4, 8])
        SC = sb("SC", [128, 4, 8])
        S1 = sb("S1", [128, 4])
        CB = sb("CB", [128, 4, 8])
        CMP = XPf[:, 0:256].rearrange("p (t a b) -> p t a b", t=4, a=8)
        CM2 = XPf[:, 256:512].rearrange("p (t a b) -> p t a b", t=4, a=8)

        def experts(p):
            xnT, x_r = yield from normed([4 * p + k for k in range(4)])
            yield
            b, fr = yield from grab(PS)
            for k in range(4):
                d = mm(b[:, k * 8:k * 8 + 8], xnT[:, k * 128:(k + 1) * 128], wr, x_r, l_wr, *fr)
            yield
            r = cp(LG[:, :, :], b[:, 0:32].rearrange("p (t e) -> p t e", t=4), d, f.get("cb"))
            PS.give(b, r)
            d = red(S1[:, :], LG[:, :, :], ALU.max, r)
            d = tt(LG[:, :, :], LG[:, :, :], S1[:, :].unsqueeze(2).to_broadcast([128, 4, 8]), ALU.subtract, d)
            d = ac(SC[:, :, :], LG[:, :, :], ACT.Exp, d)
            yield
            d = red(S1[:, :], SC[:, :, :], ALU.add, d)
            d = dve.put(lambda e: e.reciprocal(S1[:, :], S1[:, :]), (d,))
            d_s = tt(SC[:, :, :], SC[:, :, :], S1[:, :].unsqueeze(2).to_broadcast([128, 4, 8]), ALU.mult, d)
            other = SC[:, :, :].unsqueeze(2).to_broadcast([128, 4, 8, 8])
            own = SC[:, :, :].unsqueeze(3).to_broadcast([128, 4, 8, 8])
            d1 = tt(CMP, other, own, ALU.is_ge, d_s, last)
            d2 = tt(CM2, other, own, ALU.is_gt, d_s, last)
            for t in range(4):
                d = tt(CMP[:, t], CMP[:, t], tri[:, 0], ALU.mult, d1, l_tri)
                d2 = tt(CM2[:, t], CM2[:, t], tri[:, 1], ALU.mult, d2)
            d = tt(CMP, CMP, CM2, ALU.add, d2)
            d = red(CB[:, :, :], CMP, ALU.add, d)
            d = stt(CB[:, :, :], CB[:, :, :], 1.5, SC[:, :, :], ALU.is_lt, ALU.mult, d)
            d = red(S1[:, :], CB[:, :, :], ALU.add, d)
            d = ts(S1[:, :], S1[:, :], 1.1920928955078125e-07, None, ALU.add, None, d)
            d = dve.put(lambda e: e.reciprocal(S1[:, :], S1[:, :]), (d,))
            cb_r = tt(CB[:, :, :], CB[:, :, :], S1[:, :].unsqueeze(2).to_broadcast([128, 4, 8]), ALU.mult, d)

            def down(ex, hbs):
                b, fr = yield from grab(PS)
                for k in range(4):
                    for j in range(4):
                        d = mm(b[:, k * 128:(k + 1) * 128], hbs[j][0][:, k * 128:(k + 1) * 128], wd[:, ex, j, :],
                               hbs[j][1], l_wd, *fr, start=j == 0, stop=j == 3)
                    if k == 1:
                        yield
                for j in range(4):
                    HB.give(hbs[j][0], d)
                yield
                for k in range(4):
                    t = 4 * p + k
                    x_w[t] = stt(X[:, t, :], b[:, k * 128:(k + 1) * 128], CB[:, k, ex:ex + 1], X[:, t, :],
                                 ALU.mult, ALU.add, d, cb_r, x_w[t])
                PS.give(b, x_w[t])

            prev = None
            for ex in range(NE):
                hbs = []
                for j in range(4):
                    (bg, fg), (bu, fu) = yield from grab(PS, 2)
                    dg = mm(bg[:, :], wg[:, ex, j * 128:(j + 1) * 128], xnT, x_r, l_wg, *fg)
                    du = mm(bu[:, :], wu[:, ex, j * 128:(j + 1) * 128], xnT, l_wu, *fu)
                    rg, rfr = yield from grab(TB)
                    yield
                    r = ac(rg, bg[:, :], ACT.Relu, dg, *rfr)
                    PS.give(bg, r)
                    hb, hfr = yield from grab(HB)
                    d = tt(hb, bu[:, :], rg, ALU.mult, du, r, *hfr)
                    PS.give(bu, d)
                    TB.give(rg, d)
                    hbs.append((hb, d))
                if prev:
                    yield from down(ex - 1, prev)
                prev = hbs
            XT.give(xnT, du)
            yield from down(NE - 1, prev)
            f["cb"] = x_w[4 * p + 3]
            for k in range(4):
                t = 4 * p + k
                count["out"] += 16
                sp.put(lambda e, o=out_d[t // 2, (t % 2) * 128:(t % 2) * 128 + 128, :], a=X[:, t, :]: e.dma_start(o, a),
                       (x_w[t],), s_out, count["out"])

        run(*(signed(p) for p in range(NP)))
        todo, done, moe = list(range(NB)), set(), list(range(NP))
        active, slots, ex = [], [0, 1], None
        while todo or active or moe or ex:
            if todo and slots:
                b8 = todo.pop(0)
                active.append((attend(b8, slots[0]), slots.pop(0), b8))
            if ex is None and moe and {2 * moe[0], 2 * moe[0] + 1} <= done:
                ex = experts(moe.pop(0))
            for a in list(active):
                if next(a[0], "end") == "end":
                    active.remove(a)
                    slots.append(a[1])
                    done.add(a[2])
            if ex is not None and next(ex, "end") == "end":
                ex = None

        for q in (pe, act, dve, pool, sp):
            q.number()
        block = ctx.enter_context(nc.Block())

        @block.tensor
        def _(e):
            pe.emit(e)

        @block.scalar
        def _(e):
            act.emit(e)

        @block.vector
        def _(e):
            dve.emit(e)

        @block.gpsimd
        def _(e):
            pool.emit(e)

        @block.sync
        def _(e):
            sp.emit(e)
            e.wait_ge(s_out, count["out"])


def kernel(**inputs):
    import numpy as np
    import concourse.bacc as _bacc
    from concourse import mybir as _mybir
    from concourse.bass_utils import run_bass_kernel_spmd as _run

    i = {k: np.asarray(v) for k, v in inputs.items()}
    c = np.ascontiguousarray
    f4 = np.float32
    r = np.arange(128)
    arrays = {
        "x": i["L0_attn_x"],
        "wqkv": np.concatenate([i["L0_attn_Wq"].T, i["L0_attn_Wk"].T, i["L0_attn_Wv"].T], axis=1),
        "conv": np.concatenate([i["L0_attn_conv_q"], i["L0_attn_conv_k"], i["L0_attn_conv_v"]]).reshape(32, 128, 4).transpose(1, 0, 2),
        "wab": np.concatenate([i["L0_attn_Wa"].T, i["L0_attn_Wb"].T], axis=1),
        "gate": np.stack([i["L0_attn_A_log"], i["L0_attn_dt_bias"]], axis=1),
        "wo": i["L0_attn_Wo"].T.reshape(16, 128, 128).transpose(1, 0, 2),
        "sgn": i["L0_ffn_weight"].T,
        "awq": i["L1_attn_wq"].T.reshape(128, 4, 4, 8).transpose(0, 2, 1, 3).reshape(128, 16, 8),
        "awk": i["L1_attn_wk"].T.reshape(128, 4, 8),
        "awv": i["L1_attn_wv"].T,
        "awo": i["L1_attn_wo"].T,
        "wr": i["L1_ffn_Wr"].T,
        "wg": i["L1_ffn_Wg"].transpose(2, 0, 1),
        "wu": i["L1_ffn_Wu"].transpose(2, 0, 1),
        "wd": i["L1_ffn_Wd"].transpose(2, 0, 1).reshape(4, 128, 8, 128).transpose(1, 2, 0, 3),
    }
    s, t = r[:, None], r[None, :]
    lm = np.zeros((128, 6, 64), f4)
    for lv in range(6):
        m = 1 << lv
        a, b = (s % 64) // m, t[:, :64] // m
        lm[:, lv, :] = (a % 2 == 1) & (b == a - 1)
    lm[:, 0, :] = (s % 2 == 0) & (t[:, :64] == s % 64 + 1)
    sel = np.zeros((128, 8, 16), f4)
    for k in range(8):
        sel[:, k, :] = np.arange(16)[None, :] == 2 * k + s // 64
    reset = np.ones((16, 512), f4)
    reset[:, ::256] = 0
    e = np.arange(8)
    tri = np.stack([e[None, :] < e[:, None], e[None, :] > e[:, None]]).astype(f4)
    arrays |= {
        "ident": np.eye(128, dtype=f4),
        "idp": (s % 64 == t[:, :64]).astype(f4),
        "emask": np.concatenate([np.where(t <= s, f4(-1e30), f4(0)), np.where(t < s, f4(-1e30), f4(0))], axis=1),
        "lmask": lm,
        "sel": sel,
        "reset": reset,
        "tri": np.broadcast_to(tri, (128, 2, 8, 8)),
    }
    nc = _bacc.Bacc("TRN2", target_bir_lowering=False, num_devices=1)
    arrays = {f"in_{k}_dram": c(v) for k, v in arrays.items()}
    args = [nc.dram_tensor(k, v.shape, _mybir.dt.from_np(v.dtype), kind="ExternalInput").ap() for k, v in arrays.items()]
    out = nc.dram_tensor("out_0_dram", (NB, T, D), _mybir.dt.float32, kind="ExternalOutput").ap()
    program(nc, *args, out)
    res = _run(nc, [arrays], core_ids=[0])
    return res.results[0]["out_0_dram"]
```
